# Optimizing a Trainium2 kernel written in Bass

```python
import numpy as np
import jax
import jax.numpy as jnp

def _softmax(x, axis=-1):
    return jax.nn.softmax(x, axis=axis)

def _gelu(x):
    return jax.nn.gelu(x, approximate=True)

def _silu(x):
    return jax.nn.silu(x)

def _sigmoid(x):
    return jax.nn.sigmoid(x)

def _layernorm(x, axis=-1, eps=1e-05):
    m = jnp.mean(x, axis=axis, keepdims=True)
    v = jnp.var(x, axis=axis, keepdims=True)
    return (x - m) / jnp.sqrt(v + eps)

def _scatter_add(tgt, idx, src, axis=0):
    return tgt.at[idx].add(src)

def _segment_sum(src, seg, n):
    return jax.ops.segment_sum(src, seg, n)
kernel_name = 'mk_flamingo_gated_d1_seqx_r8_4ade9b'

def setup_inputs(seed: int=0):
    np.random.seed(seed)
    _w = jnp.asarray

    def _rec_inputs():
        import jax
        import jax.numpy as jnp
        _rk = jax.random.key(seed)
        x = -0.0003929 + 0.9999 * jax.random.normal(jax.random.fold_in(_rk, 1), (64, 128, 128), jnp.float32)
        _lenS = 128 - jax.random.randint(jax.random.fold_in(_rk, 7), (64,), 0, max(1, 128 // 4) + 1, jnp.int32)
        _lenS2 = 77 - jax.random.randint(jax.random.fold_in(_rk, 8), (64,), 0, max(1, 77 // 4) + 1, jnp.int32)
        _ctx_768P = jax.random.normal(jax.random.fold_in(_rk, 11), (64, 16, 96), jnp.float32)
        _ctx_768c = jax.random.dirichlet(jax.random.fold_in(_rk, 511), 0.3 * jnp.ones((16,), jnp.float32), (64, 77))
        _ctx_768t = jnp.einsum('bsk,bkd->bsd', _ctx_768c, _ctx_768P)
        _ctx_768t = _ctx_768t * jax.lax.rsqrt(jnp.mean(jnp.square(_ctx_768t)) + 1e-12) * 0.953939
        ctx_768 = 0.00095986 + 0.999812 * (_ctx_768t + 0.3 * jax.random.normal(jax.random.fold_in(_rk, 611), (64, 77, 96), jnp.float32))
        _validS = jnp.arange(128)[None, :] < _lenS[:, None]
        _validS2 = jnp.arange(77)[None, :] < _lenS2[:, None]
        _causal = jnp.tril(jnp.ones((128, 128), dtype=bool))
        mask_BxS2_bf1 = jnp.ones((64, 77), dtype=bool)
        _g = jax.random.normal(jax.random.fold_in(_rk, 9001), (2, 1), jnp.float32)
        _g = jnp.sign(_g) * jnp.maximum(jnp.abs(_g), 1.0) + (_g == 0) * 1.0
        g_xattn = _g[0]
        g_ffn = _g[1]
        return (x, ctx_768, mask_BxS2_bf1, g_xattn, g_ffn)
    x, ctx_768, mask_BxS2_bf1, g_xattn, g_ffn = _rec_inputs()

    def _L0_xattn_setup():
        import jax, jax.numpy as jnp
        import numpy as np
        DIM = 128
        CTX_DIM = 96
        HEADS = 16
        key = jax.random.key(seed)
        ks = jax.random.split(key, 7)
        B, N, M = (4, 512, 32)
        x = jax.random.normal(ks[0], (B, N, DIM), dtype=jnp.float32)
        context = jax.random.normal(ks[1], (B, M, CTX_DIM), dtype=jnp.float32)
        context_mask = jnp.ones((B, M), dtype=bool)
        s_d = 1.0 / np.sqrt(DIM)
        s_c = 1.0 / np.sqrt(CTX_DIM)
        Wq = jax.random.normal(ks[2], (DIM, DIM), dtype=jnp.float32) * s_d
        Wk = jax.random.normal(ks[3], (CTX_DIM, DIM), dtype=jnp.float32) * s_c
        Wv = jax.random.normal(ks[4], (CTX_DIM, DIM), dtype=jnp.float32) * s_c
        Wo = jax.random.normal(ks[5], (DIM, DIM), dtype=jnp.float32) * s_d
        return {'x': x, 'context': context, 'context_mask': context_mask, 'Wq': Wq, 'Wk': Wk, 'Wv': Wv, 'Wo': Wo}
    _L0_xattn_all = _L0_xattn_setup()
    _L0_xattn_in = {k: v for k, v in _L0_xattn_all.items() if k in ('Wq', 'Wk', 'Wv', 'Wo')}
    del _L0_xattn_all

    def _L0_ffn_setup():
        import jax, jax.numpy as jnp
        import numpy as np
        B, S, H, I, E, K = (2, 256, 128, 256, 8, 2)
        key = jax.random.key(seed)
        k1, k2, k3, k4, k5 = jax.random.split(key, 5)
        scale_h = 1.0 / np.sqrt(H)
        scale_i = 1.0 / np.sqrt(I)
        return {'x': jax.random.normal(k1, (B, S, H), dtype=jnp.float32), 'Wg': jax.random.normal(k2, (H, E), dtype=jnp.float32) * scale_h, 'W11': jax.random.normal(k3, (E, H, I), dtype=jnp.float32) * scale_h, 'W12': jax.random.normal(k4, (E, H, I), dtype=jnp.float32) * scale_h, 'W2': jax.random.normal(k5, (E, I, H), dtype=jnp.float32) * scale_i}
    _L0_ffn_all = _L0_ffn_setup()
    _L0_ffn_in = {k: v for k, v in _L0_ffn_all.items() if k in ('Wg', 'W11', 'W12', 'W2')}
    del _L0_ffn_all
    return {'x': x, 'ctx_768': ctx_768, 'mask_BxS2_bf1': mask_BxS2_bf1, 'g_xattn': g_xattn, 'g_ffn': g_ffn, 'L0_xattn_Wq': _L0_xattn_in['Wq'], 'L0_xattn_Wk': _L0_xattn_in['Wk'], 'L0_xattn_Wv': _L0_xattn_in['Wv'], 'L0_xattn_Wo': _L0_xattn_in['Wo'], 'L0_ffn_Wg': _L0_ffn_in['Wg'], 'L0_ffn_W11': _L0_ffn_in['W11'], 'L0_ffn_W12': _L0_ffn_in['W12'], 'L0_ffn_W2': _L0_ffn_in['W2']}

def reference(x, ctx_768, mask_BxS2_bf1, g_xattn, g_ffn, L0_xattn_Wq, L0_xattn_Wk, L0_xattn_Wv, L0_xattn_Wo, L0_ffn_Wg, L0_ffn_W11, L0_ffn_W12, L0_ffn_W2):
    import jax
    import jax.numpy as jnp

    def _L0_xattn_ref(x, context, context_mask, Wq, Wk, Wv, Wo):
        import jax, jax.numpy as jnp
        import numpy as np
        DIM = 128
        CTX_DIM = 96
        HEADS = 16
        B, N, _ = x.shape
        M = context.shape[1]
        hd = DIM // HEADS
        scale = hd ** (-0.5)
        q = (x @ Wq).reshape(B, N, HEADS, hd).transpose(0, 2, 1, 3)
        k = (context @ Wk).reshape(B, M, HEADS, hd).transpose(0, 2, 1, 3)
        v = (context @ Wv).reshape(B, M, HEADS, hd).transpose(0, 2, 1, 3)
        scores = jnp.einsum('bhid,bhjd->bhij', q, k) * scale
        max_neg = -jnp.finfo(scores.dtype).max
        scores = jnp.where(context_mask[:, None, None, :], scores, max_neg)
        attn = jax.nn.softmax(scores, axis=-1)
        out = jnp.einsum('bhij,bhjd->bhid', attn, v)
        out = out.transpose(0, 2, 1, 3).reshape(B, N, DIM)
        return out @ Wo

    def _L0_ffn_ref(x, Wg, W11, W12, W2):
        import jax, jax.numpy as jnp
        import numpy as np
        B, S, H, I, E, K = (2, 256, 128, 256, 8, 2)
        gate_scores = jax.nn.softmax(x @ Wg, axis=-1)
        topk_scores, topk_idx = jax.lax.top_k(gate_scores, K)
        topk_scores = topk_scores / (topk_scores.sum(-1, keepdims=True) + 1e-08)
        gate = jnp.einsum('bsh,ehi->bsei', x, W11)
        value = jnp.einsum('bsh,ehi->bsei', x, W12)
        fused = gate * jax.nn.sigmoid(gate) * value
        expert_out = jnp.einsum('bsei,eih->bseh', fused, W2)
        gathered = jnp.take_along_axis(expert_out, topk_idx[..., None], axis=2)
        out = jnp.sum(topk_scores[..., None] * gathered, axis=2)
        return out
    x = x + jnp.tanh(g_xattn[0]) * _L0_xattn_ref(_layernorm(x, axis=-1), ctx_768, mask_BxS2_bf1, L0_xattn_Wq, L0_xattn_Wk, L0_xattn_Wv, L0_xattn_Wo)
    x = x + jnp.tanh(g_ffn[0]) * _L0_ffn_ref(_layernorm(x, axis=-1), L0_ffn_Wg, L0_ffn_W11, L0_ffn_W12, L0_ffn_W2)
    return x

_drawn_inputs = setup_inputs


def setup_inputs(seed=0):
    import zlib

    import numpy as np

    out = dict(_drawn_inputs(seed))
    spreads = {}
    factors = {}
    for name, (base, spread) in spreads.items():
        noise = np.random.default_rng([zlib.crc32(name.encode()), seed]).standard_normal(out[name].shape)
        drawn = base * np.exp(spread * noise) if base else spread * noise
        out[name] = jnp.asarray(drawn.astype(out[name].dtype))
    for name, factor in factors.items():
        out[name] = (out[name] * factor).astype(out[name].dtype)
    return out
```

```python
from contextlib import ExitStack

import concourse.bass as bass
from concourse import mybir

P = 128
ALU = mybir.AluOpType
ACT = mybir.ActivationFunctionType
F32 = mybir.dt.float32
BF16 = mybir.dt.bfloat16
U8 = mybir.dt.uint8
AX_X = mybir.AxisListType.X

HEADS = 16
TOPK = 2
U32 = mybir.dt.uint32
I32 = mybir.dt.int32
HD = 8
GROUPS = 4
HPG = HEADS // GROUPS
KA = 64
UNROLL = 4
LN_EPS = 1e-5
GATE_EPS = 1e-8
MASKED = 3.3895313892515355e38


def flamingo_block(nc, x, ctx_in, mask, g_xattn, g_ffn, wq, wk, wv, wo, wg, w11, w12, w2, out):
    NB, T, D = x.shape
    C = ctx_in.shape[1]
    M = mask.shape[1]
    E, _, I = w11.shape
    KB = M - KA
    HPC = 8
    RB = HPC * KB
    NC_A = HEADS // 2
    NC_B = HEADS // HPC
    SW = HPG * M
    VW = HD + 1
    IC = I // P
    NTOK = NB * T
    TILES_PAD = E
    TILES = TOPK * NTOK // P + E
    SCALE = float(HD) ** -0.5
    assert T == P and D == P and HEADS * HD == D and RB <= P and SW <= 512

    with ExitStack() as es:
        def sb(name, shape, dt=F32):
            return es.enter_context(nc.sbuf_tensor(name, shape, dt))

        def sem(name):
            return es.enter_context(nc.semaphore(name))

        x_all = sb("x_all", [P, NB, D])
        m8_all = sb("m8_all", [P, NB, E])
        wq_s = sb("wq_s", [P, D])
        wk_s = sb("wk_s", [P, D])
        wv_s = sb("wv_s", [P, D])
        wo_s = sb("wo_s", [P, D])
        wg_s = sb("wg_s", [P, E])
        w1_s = sb("w1_s", [P, E, 2 * I])
        w2_s = sb("w2_s", [P, E, IC, D])
        gains = sb("gains", [P, 2])
        ident = sb("ident", [P, P])
        SLOTS = NTOK + P
        ROW = D + 4
        expert_in = nc.dram_tensor("expert_in", [E * SLOTS + TILES_PAD * P, ROW], F32, kind="Internal")
        expert_out = nc.dram_tensor("expert_out", [TOPK * NTOK, D], F32, kind="Internal")
        pay = sb("pay", [P, UNROLL, TOPK, ROW])

        PADDING = 1 << 20
        padrow = sb("padrow", [P, ROW])
        eoff = sb("eoff", [P, E])
        etab = sb("etab", [P, 8, E])
        eint = sb("eint", [P, 3, E], I32)
        lower = sb("lower", [P, E, E])
        iota_t = sb("iota_t", [P, TILES])
        past = sb("past", [P, TILES, E])
        pastr = sb("pastr", [P, TILES, E])
        tile_f = sb("tile_f", [P, 3, TILES])
        tile_i = sb("tile_i", [P, 2, TILES], I32)
        gate_d = sb("gate_d", [P, NB, E])
        gate_s = sb("gate_s", [P, 3, NB])
        gate_w = sb("gate_w", [P, TOPK, NB])
        xe = sb("xe", [P, 8, ROW])
        xeT = sb("xeT", [P, 2, P])
        sg = sb("sg", [P, 2, I])
        ff = sb("ff", [P, 4, I])
        ffT = sb("ffT", [P, 2, I])
        ye = sb("ye", [P, 4, D])
        to = sb("to", [P, 4, 1], U32)
        no_row = sb("no_row", [P, 1], U32)
        CB = 8
        yk = sb("yk", [P, 2, TOPK, CB, D])

        mask_u8 = sb("mask_u8", [P, NB * M], U8)
        mask_b = sb("mask_b", [P, NB, M], BF16)
        ones_b = sb("ones_b", [P, P], BF16)
        band = sb("band", [P, HEADS])
        khead = sb("khead", [P, HPG])
        vhead = sb("vhead", [P, 2, HEADS])
        neg_half = sb("neg_half", [P, 2])
        eps = sb("eps", [P, 2])
        ctxT = sb("ctxT", [C, UNROLL, 2 * P])
        xn1 = sb("xn1", [P, 2, D])
        xn2 = sb("xn2", [P, 2, D])
        xt = sb("xt", [P, 2, 2 * P])
        vkq = sb("vkq", [P, 2, 2 * D + M + P])
        kbd = sb("kbd", [P, 2, HPG, M])
        vbd = sb("vbd", [P, UNROLL, 2, HEADS, VW])
        mrow = sb("mrow", [P, 2, M], BF16)
        prob = sb("prob", [P, 2, HEADS * M])
        smax = sb("smax", [P, 2, HEADS])
        probT = sb("probT", [P, 8 * P + 2 * P + P])
        rden = sb("rden", [P, 2, HEADS])
        onorm = sb("onorm", [P, 2, HEADS, HD])
        bnst = sb("bnst", [P, 2, 2, 6])
        mv = sb("mv", [P, UNROLL, 2, 2])
        vare = sb("vare", [P, UNROLL, 2])
        rstd = sb("rstd", [P, UNROLL, 2])
        lrt = sb("lrt", [P, 2, 3, E])
        m8 = sb("m8", [P, 2, E])
        ix8 = sb("ix8", [P, 2, E], U32)
        pick = sb("pick", [P, 2, TOPK, E], BF16)
        iota_e = sb("iota_e", [P, TOPK, E])
        nextrow = sb("nextrow", [P, E])
        row8 = sb("row8", [P, 2, E])
        prow = sb("prow", [P, 2, TOPK, E])
        dest = sb("dest", [P, 2, TOPK], U32)
        ustri = sb("ustri", [P, P], BF16)
        turn_add = sb("turn_add", [P, TOPK], U32)

        s_x = [sem(f"s_x{i}") for i in range(4)]
        s_w = sem("s_w")
        s_wffn = sem("s_wffn")
        s_mask = sem("s_mask")
        s_ctx = [sem(f"s_ctx{i}") for i in range(UNROLL)]
        s_g = sem("s_g")
        const_pool = sem("const_pool")
        const_dve = sem("const_dve")
        const_act = sem("const_act")
        sc_done = sem("sc_done")
        sub_done = sem("sub_done")
        max_done = sem("max_done")
        exp_done = sem("exp_done")
        vkq_done = sem("vkq_done")
        vkq_copied = sem("vkq_copied")
        pa_done = sem("pa_done")
        pb_done = sem("pb_done")
        pc_done = sem("pc_done")
        pa_copied = sem("pa_copied")
        pb_copied = sem("pb_copied")
        pc_copied = sem("pc_copied")
        xt_done = sem("xt_done")
        xt_copied = sem("xt_copied")
        pv_done = sem("pv_done")
        wo_done = sem("wo_done")
        rden_done = sem("rden_done")
        onorm_done = sem("onorm_done")
        wo_taken = sem("wo_taken")
        x1_done = sem("x1_done")
        m8_kept = sem("m8_kept")
        max8_done = sem("max8_done")
        ix8_done = sem("ix8_done")
        pick_done = sem("pick_done")
        row8_done = sem("row8_done")
        prow_done = sem("prow_done")
        next_done = sem("next_done")
        dest_done = sem("dest_done")
        pay_done = sem("pay_done")
        tok_done = sem("tok_done")
        scat = [sem(f"scat{i}") for i in range(UNROLL)]
        s_pad = sem("s_pad")
        s_tail = sem("s_tail")
        s_tab = sem("s_tab")
        s_gate = sem("s_gate")
        xe_in = [sem(f"xe_in{i}") for i in range(8)]
        xe_done = sem("xe_done")
        xe_copied = sem("xe_copied")
        h_done = sem("h_done")
        silu_done = sem("silu_done")
        f_done = sem("f_done")
        ft_done = sem("ft_done")
        ft_copied = sem("ft_copied")
        y_done = sem("y_done")
        y_copied = sem("y_copied")
        to_done = sem("to_done")
        y_out = [sem(f"y_out{i}") for i in range(4)]
        s_y = [sem(f"s_y{i}") for i in range(2)]
        s_sum = sem("s_sum")
        s_out = sem("s_out")
        s_half_sum = sem("s_half_sum")
        bn1_done = sem("bn1_done")
        bn2_done = sem("bn2_done")
        mv_done = sem("mv_done")
        var_done = sem("var_done")
        rstd_done = sem("rstd_done")
        xn1_done = sem("xn1_done")
        xn2_done = sem("xn2_done")
        kbd_done = sem("kbd_done")
        vbd_done = sem("vbd_done")
        mrow_done = sem("mrow_done")

        class Plan:
            def __init__(self, total, unroll, first, loop0, loop1, last):
                assert first % unroll == 0 and loop0 % unroll == 0 and loop1 % unroll == 0
                self.total, self.unroll, self.first, self.loop0, self.loop1, self.last = total, unroll, first, loop0, loop1, last

        class Step:
            def __init__(self, plan, j, off, looped):
                self.plan, self.j, self.off, self.looped = plan, j, off, looped

            def has(self, lag):
                return self.looped or 0 <= self.plan.unroll * self.j + self.off + lag < self.plan.total

            def n(self, k):
                return self.j * self.plan.unroll + (self.off + k)

            def par(self, lag):
                return (self.off + lag) % 2

            def slot(self, lag, ring=4):
                return (self.off + lag) % ring

            def turn(self, lag, ring=4):
                return self.j * (self.plan.unroll // ring) + (self.off + lag) // ring

        def run(eng, plan, step, before_loop=lambda: None):
            u = plan.unroll
            for s in range(plan.first, plan.loop0):
                step(Step(plan, s // u, s % u, False))
            before_loop()
            with eng.Fori(plan.loop0 // u, plan.loop1 // u) as j:
                for off in range(u):
                    step(Step(plan, j, off, True))
            for s in range(plan.loop1, plan.last + 1):
                step(Step(plan, s // u, s % u, False))

        FIRST, LOOP0 = -UNROLL, 3 * UNROLL
        attend = Plan(NB, UNROLL, FIRST, LOOP0, NB - 2 * UNROLL, NB + 7)
        experts = Plan(TILES, 8, -8, 8, TILES - 8, TILES + 3)

        LAGS = {
            sc_done: (0,), max_done: (0,), sub_done: (0,), exp_done: (-1,), vkq_done: (2,), vkq_copied: (2,),
            pa_done: (-1,), pb_done: (-1,), pc_done: (-1, -2), pa_copied: (-1,), pb_copied: (-1,), pc_copied: (-1, -2),
            xt_done: (3, -4), xt_copied: (3, -4), pv_done: (-1,), wo_done: (-2, -6), rden_done: (-2,), onorm_done: (-2,),
            x1_done: (-3,), wo_taken: (4, -7), bn1_done: (4,), bn2_done: (-3,), mv_done: (4, -3), var_done: (4, -3),
            rstd_done: (4, -3), xn1_done: (3,), xn2_done: (-4,), pay_done: (-6,), max8_done: (-6,), ix8_done: (-6,),
            m8_kept: (-6,), pick_done: (-6,), row8_done: (-7,), prow_done: (-7,), next_done: (-7,), dest_done: (-8,),
            tok_done: (-8,), kbd_done: (2,), vbd_done: (1,), mrow_done: (2,),
            xe_done: (2,), xe_copied: (2,), h_done: (0,), silu_done: (0,), f_done: (0,), ft_done: (-2,), ft_copied: (-2,),
            y_done: (-3,), y_copied: (-3,), to_done: (-3,),
        }

        def need(eng, s, signal, step=0):
            first, last = max(LAGS[signal]), min(LAGS[signal])
            if s.looped:
                eng.wait_ge(signal, s.n(step + first + 1))
                return
            count = min(s.n(step) + first + 1, s.plan.total + first - last)
            if count > 0:
                eng.wait_ge(signal, count)

        def batch(t, s, lag):
            return t[:, bass.ds(s.n(lag), 1)] if s.looped else t[:, s.n(lag):s.n(lag) + 1]

        def rows(t, s, lag):
            return batch(t, s, lag).rearrange("p a d -> p (a d)")

        XC = [0, LOOP0 + 4, 29, 46, NB]
        OB = 8

        with ExitStack() as ps_es:
            def pb(name, shape, dt=F32):
                return ps_es.enter_context(nc.psum_tensor(name, shape, dt))
            ps_s = pb("ps_s", [P, GROUPS, 512])
            ps_ao = pb("ps_ao", [P, 512])
            ps_bw = pb("ps_bw", [P, 512])
            ps_c = pb("ps_c", [P, 512])
            ps_t = pb("ps_t", [P, 512])
            block = ps_es.enter_context(nc.Block())

            @block.sync
            def _(sp):
                for k in range(4):
                    sp.dma_start(x_all[:, XC[k]:XC[k + 1], :],
                                 x[XC[k]:XC[k + 1], :, :].rearrange("b t d -> t b d")).then_inc(s_x[k], 16)
                    if k == 0:
                        for dst, src in ((wk_s[0:C, :], wk), (wv_s[0:C, :], wv), (wq_s[:, :], wq),
                                         (wo_s[:, :], wo), (wg_s[:, :], wg)):
                            sp.dma_start(dst, src).then_inc(s_w, 16)
                sp.dma_start(w1_s[:, :, 0:I], w11.rearrange("e h i -> h e i")).then_inc(s_wffn, 16)
                sp.dma_start(w1_s[:, :, I:2 * I], w12.rearrange("e h i -> h e i")).then_inc(s_wffn, 16)
                for e in range(E):
                    sp.dma_start(w2_s[:, e, :, :], w2[e, :, :].rearrange("(c i) h -> i c h", c=IC)).then_inc(s_wffn, 16)
                sp.wait_ge(s_pad, 2)
                for k in range(TILES_PAD):
                    sp.dma_start(expert_in[E * SLOTS + k * P:E * SLOTS + (k + 1) * P, :], padrow[:, :]).then_inc(s_tail, 16)

            @block.gpsimd
            def _(pool):
                pool.memset(ident[:, :], 0.0).then_inc(const_pool, 1)
                pool.memset(band[:, :], 1.0).then_inc(const_pool, 1)
                pool.memset(vhead[:, :, :], 1.0).then_inc(const_pool, 1)
                pool.memset(ustri[:, :], 1.0).then_inc(const_pool, 1)
                pool.memset(ones_b[:, :], 1.0).then_inc(const_pool, 1)
                pool.memset(eps[:, :], LN_EPS)
                pool.memset(neg_half[:, :], -0.5).then_inc(const_pool, 1)
                pool.memset(vbd[:, :, :, :, :], 1.0).then_inc(const_pool, 1)
                pool.wait_ge(const_pool, 7)
                pool.affine_select(out=ident[:, :], in_=ident[:, :], compare_op=ALU.not_equal, fill=1.0,
                                   base=0, pattern=[[-1, P]], channel_multiplier=1).then_inc(const_pool, 1)
                pool.affine_select(out=band[:, :], in_=band[:, :], compare_op=ALU.is_ge, fill=0.0,
                                   base=0, pattern=[[-HD, HEADS]], channel_multiplier=1).then_inc(const_pool, 1)
                pool.wait_ge(const_pool, 9)
                pool.affine_select(out=band[:, :], in_=band[:, :], compare_op=ALU.is_ge, fill=0.0,
                                   base=HD - 1, pattern=[[HD, HEADS]], channel_multiplier=-1).then_inc(const_pool, 1)
                v = vhead[:, 0, :].rearrange("p (a b) -> p a b", b=2)
                pool.affine_select(out=v[:, :, 0:1], in_=v[:, :, 0:1], compare_op=ALU.is_ge, fill=0.0,
                                   base=KA - 1, pattern=[[0, HEADS // 2], [0, 1]], channel_multiplier=-1).then_inc(const_pool, 1)
                pool.affine_select(out=v[:, :, 1:2], in_=v[:, :, 1:2], compare_op=ALU.is_ge, fill=0.0,
                                   base=-KA, pattern=[[0, HEADS // 2], [0, 1]], channel_multiplier=1).then_inc(const_pool, 1)
                w = vhead[:, 1, :].rearrange("p (a b) -> p a b", b=HPC)
                pool.affine_select(out=w, in_=w, compare_op=ALU.is_ge, fill=0.0,
                                   base=0, pattern=[[0, NC_B], [-KB, HPC]], channel_multiplier=1).then_inc(const_pool, 1)
                pool.wait_ge(const_pool, 13)
                pool.affine_select(out=w, in_=w, compare_op=ALU.is_ge, fill=0.0,
                                   base=KB - 1, pattern=[[0, NC_B], [KB, HPC]], channel_multiplier=-1).then_inc(const_pool, 1)
                pool.wait_ge(const_pool, 14)
                for r in range(UNROLL):
                    pool.tensor_copy(out=vbd[:, r, :, :, HD], in_=vhead[:, :, :]).then_inc(const_pool, 1)

                pool.affine_select(out=ustri[:, :], in_=ustri[:, :], compare_op=ALU.is_ge, fill=0.0,
                                   base=-1, pattern=[[1, P]], channel_multiplier=-1).then_inc(const_pool, 1)
                pool.iota(iota_e[:, :, :], pattern=[[0, TOPK], [1, E]], base=0, channel_multiplier=0,
                          allow_small_or_imprecise_dtypes=True).then_inc(const_pool, 1)
                pool.iota(nextrow[:, :], pattern=[[SLOTS, E]], base=0, channel_multiplier=0,
                          allow_small_or_imprecise_dtypes=True).then_inc(const_pool, 1)
                pool.memset(turn_add[:, :], UNROLL * T).then_inc(const_pool, 1)
                pool.memset(padrow[:, 0:D], 0.0).then_inc(s_pad, 1)
                pool.memset(padrow[:, D:ROW].bitcast(U32), PADDING).then_inc(s_pad, 1)
                pool.iota(eoff[:, :], pattern=[[SLOTS, E]], base=0, channel_multiplier=0,
                          allow_small_or_imprecise_dtypes=True).then_inc(s_pad, 1)
                pool.iota(iota_t[:, :], pattern=[[1, TILES]], base=0, channel_multiplier=0,
                          allow_small_or_imprecise_dtypes=True).then_inc(s_pad, 1)
                pool.memset(lower[:, :, :], 1.0).then_inc(s_pad, 1)
                pool.memset(no_row[:, :], 0)
                pool.wait_ge(s_pad, 5)
                pool.affine_select(out=lower[:, :, :], in_=lower[:, :, :], compare_op=ALU.is_ge, fill=0.0,
                                   base=0, pattern=[[1, E], [-1, E]], channel_multiplier=0).then_inc(s_pad, 1)
                pool.memset(pay[:, :, :, :], 0.0).then_inc(const_pool, 1)
                pool.wait_ge(const_pool, 14 + UNROLL + 5)
                for r in range(UNROLL):
                    pool.iota(pay[:, r, :, D:D + 1].bitcast(I32), pattern=[[NTOK, TOPK]], base=(r - UNROLL) * T, channel_multiplier=1,
                              allow_small_or_imprecise_dtypes=True).then_inc(const_pool, 1)
                CONSTS = 14 + UNROLL + 5 + UNROLL
                pool.wait_ge(const_pool, CONSTS)
                pool.wait_ge(const_dve, 4)

                def step(s):
                    if s.has(2):
                        need(pool, s, sc_done)
                        pool.tensor_copy(out=mrow[:, s.par(2), :], in_=rows(mask_b, s, 2)).then_inc(mrow_done, 1)
                    if s.has(4) or s.has(-3):
                        k = s.slot(0)
                        need(pool, s, mv_done)
                        pool.tensor_tensor(out=vare[:, k, :], in0=mv[:, k, :, 1], in1=eps[:, :], op=ALU.add).then_inc(var_done, 1)
                        need(pool, s, var_done)
                        pool.tensor_tensor(out=rstd[:, k, :], in0=vare[:, k, :], in1=neg_half[:, :],
                                           op=ALU.pow).then_inc(rstd_done, 1)
                    if s.has(-7):
                        k = s.par(-7)
                        need(pool, s, wo_taken)
                        need(pool, s, next_done, -1)
                        pool.tensor_tensor(out=row8[:, k, :], in0=lrt[:, s.par(0), 1, :], in1=nextrow[:, :], op=ALU.add).then_inc(row8_done, 1)
                        need(pool, s, row8_done)
                        pool.tensor_tensor(out=prow[:, k, :, :], in0=pick[:, k, :, :],
                                           in1=row8[:, k, :].unsqueeze(1).to_broadcast([P, TOPK, E]), op=ALU.mult).then_inc(prow_done, 1)
                        need(pool, s, prow_done)
                        pool.tensor_tensor(out=nextrow[:, :], in0=nextrow[:, :], in1=lrt[:, s.par(0), 2, :], op=ALU.add).then_inc(next_done, 1)
                    if s.has(-8):
                        need(pool, s, dest_done)
                        need(pool, s, pay_done, -2)
                        tok = pay[:, s.slot(-8), :, D:D + 1].bitcast(U32).rearrange("p k a -> p (k a)")
                        pool.tensor_tensor(out=tok, in0=tok, in1=turn_add[:, :], op=ALU.add).then_inc(tok_done, 1)
                    if s.has(-6):
                        need(pool, s, max8_done)
                        need(pool, s, tok_done)
                        pool.tensor_copy(out=rows(m8_all, s, -6), in_=m8[:, s.par(-6), :]).then_inc(m8_kept, 1)
                    if s.has(-8):
                        if not s.has(-6):
                            need(pool, s, tok_done)
                        for c in range(TOPK):
                            pool.indirect_dma_start(out=expert_in[:, :],
                                                    out_offset=bass.IndirectOffsetOnAxis(ap=dest[:, s.par(-8), c:c + 1], axis=0),
                                                    in_=pay[:, s.slot(-8), c, :], in_offset=None).then_inc(scat[s.slot(-8)], 16)
                    if s.has(1):
                        need(pool, s, vkq_copied, -1)
                        need(pool, s, pv_done, -2)
                        src = vkq[:, s.par(1), 0:2 * D].rearrange("p (c h d) -> p (c h) d", c=2, d=HD)
                        pool.tensor_tensor(out=vbd[:, s.slot(1), :, :, 0:HD].rearrange("p c h d -> p (c h) d"), in0=src,
                                           in1=vhead[:, :, :].rearrange("p c h -> p (c h)").unsqueeze(2).to_broadcast([P, 2 * HEADS, HD]),
                                           op=ALU.mult).then_inc(vbd_done, 1)
                    if s.has(2):
                        need(pool, s, vkq_copied)
                        kk = vkq[:, s.par(2), 2 * D:2 * D + M].unsqueeze(1).to_broadcast([P, HPG, M])
                        pool.tensor_tensor(out=kbd[:, s.par(2), :, :], in0=kk,
                                           in1=khead[:, :].unsqueeze(2).to_broadcast([P, HPG, M]),
                                           op=ALU.mult).then_inc(kbd_done, 1)

                run(pool, attend, step)
                for r in range(UNROLL):
                    pool.wait_ge(scat[r], NB // UNROLL * TOPK * 16)

            @block.scalar
            def _(act):
                act.dma_start(mask_u8[:, :], mask.rearrange("b m -> (b m)").unsqueeze(0).to_broadcast([P, NB * M])).then_inc(s_mask, 16)
                act.dma_start(gains[:, 0:1], g_xattn.unsqueeze(0).to_broadcast([P, 1])).then_inc(s_g, 16)
                act.dma_start(gains[:, 1:2], g_ffn.unsqueeze(0).to_broadcast([P, 1])).then_inc(s_g, 16)

                def load_ctx(s, lag):
                    k = s.slot(lag)
                    src = ctx_in[bass.ds(s.n(lag), 1), :, :].rearrange("a c m -> (a c) m") if s.looped else ctx_in[s.n(lag), :, :]
                    act.dma_start(ctxT[:, k, :], src).then_inc(s_ctx[k], 16)

                for b in range(FIRST + 6):
                    load_ctx(Step(attend, 0, b, False), 0)
                act.wait_ge(s_g, 32)
                act.activation(gains[:, :], gains[:, :], ACT.Tanh).then_inc(const_act, 1)

                def step(s):
                    if s.has(-1):
                        need(act, s, sub_done, -1)
                        act.activation(prob[:, s.par(-1), :], prob[:, s.par(-1), :], ACT.Exp).then_inc(exp_done, 1)
                    if s.has(2):
                        need(act, s, vkq_done)
                        need(act, s, vbd_done, -1)
                        need(act, s, kbd_done, -2)
                        act.activation(vkq[:, s.par(2), :], ps_t[:, 0:2 * D + M + P], ACT.Copy).then_inc(vkq_copied, 1)
                    if s.has(-1):
                        need(act, s, pa_done)
                        act.activation(probT[:, 0:512], ps_ao[:, :], ACT.Copy).then_inc(pa_copied, 1)
                        need(act, s, pb_done)
                        act.activation(probT[:, 512:1024], ps_bw[:, :], ACT.Copy).then_inc(pb_copied, 1)
                    if s.has(-1) or s.has(-2):
                        need(act, s, pc_done)
                        act.activation(probT[:, 1024:1408], ps_c[:, 0:384], ACT.Copy).then_inc(pc_copied, 1)
                    if s.has(3) or s.has(-4):
                        need(act, s, xt_done)
                        act.activation(xt[:, s.par(0), :], ps_t[:, 0:2 * P], ACT.Copy).then_inc(xt_copied, 1)
                    if s.has(6):
                        need(act, s, vkq_done)
                        load_ctx(s, 6)
                run(act, attend, step)

            @block.tensor
            def _(pe):
                pe.wait_ge(const_pool, 14 + UNROLL + 5)
                pe.wait_ge(s_w, 5 * 16)
                pe.wait_ge(const_dve, 2)

                def step(s):
                    if s.has(0):
                        k = s.par(0)
                        need(pe, s, vkq_copied, -2)
                        need(pe, s, kbd_done, -2)
                        need(pe, s, mrow_done, -2)
                        need(pe, s, sub_done, -1)
                        qT = vkq[:, k, 2 * D + M:]
                        for g in range(GROUPS):
                            r = 32 * g
                            pe.matmul(ps_s[:, g, 0:SW], qT[r:r + 32, :],
                                      kbd[r:r + 32, k, :, :].rearrange("p h m -> p (h m)"), start=True, stop=False)
                        for g in range(GROUPS):
                            r = 32 * g
                            last = pe.matmul(ps_s[:, g, 0:SW], ones_b[r:r + 1, :],
                                             mrow[r:r + 1, k, :].unsqueeze(1).to_broadcast([1, HPG, M]),
                                             start=False, stop=True)
                        last.then_inc(sc_done, 1)
                    if s.has(2):
                        need(pe, s, xt_copied, -1)
                        c = ctxT[:, s.slot(2), :]
                        pe.wait_ge(s_ctx[s.slot(2)], (s.turn(2) + 1) * 16)
                        pe.matmul(ps_t[:, 0:D], c[:, 0:P], wv_s[0:C, :], start=True, stop=True)
                        pe.matmul(ps_t[:, D:2 * D], c[:, P:2 * P], wv_s[0:C, :], start=True, stop=True)
                        pe.matmul(ps_t[:, 2 * D:2 * D + M], wk_s[0:C, :], c[:, KA:KA + M], start=True, stop=True)
                        pe.matmul(ps_t[:, 2 * D + M:2 * D + M + P], wq_s[:, :], xt[:, 1 - s.par(0), 0:P],
                                  start=True, stop=True).then_inc(vkq_done, 1)
                    if s.has(-1):
                        pr = prob[:, s.par(-1), :]
                        need(pe, s, exp_done)
                        need(pe, s, onorm_done)
                        for c in range(NC_A):
                            dst = (ps_ao, ps_bw)[c // 4]
                            if c == 4:
                                need(pe, s, wo_taken)
                            last = pe.transpose(dst[:, (c % 4) * P:(c % 4 + 1) * P], pr[:, c * P:(c + 1) * P], ident[:, :])
                            if c % 4 == 3:
                                last.then_inc((pa_done, pb_done)[c // 4], 1)
                    if s.has(-1) or s.has(-2):
                        need(pe, s, pc_copied, -1)
                        last = None
                        if s.has(-1):
                            for c in range(NC_B):
                                last = pe.transpose(ps_c[0:RB, c * P:(c + 1) * P], pr[:, HEADS * KA + c * RB:HEADS * KA + (c + 1) * RB], ident[:, :])
                        if s.has(-2):
                            need(pe, s, onorm_done)
                            last = pe.transpose(ps_c[:, 2 * P:3 * P],
                                                onorm[:, s.par(-2), :, :].rearrange("p h d -> p (h d)"), ident[:, :])
                        last.then_inc(pc_done, 1)
                    if s.has(3) or s.has(-4):
                        need(pe, s, vkq_copied)
                        need(pe, s, xt_copied, -1)
                        if s.has(3):
                            need(pe, s, xn1_done)
                            last = pe.transpose(ps_t[:, 0:P], xn1[:, s.par(3), :], ident[:, :])
                        if s.has(-4):
                            need(pe, s, xn2_done)
                            last = pe.transpose(ps_t[:, P:2 * P], xn2[:, s.par(-4), :], ident[:, :])
                        last.then_inc(xt_done, 1)
                    if s.has(-1):
                        need(pe, s, pa_copied)
                        need(pe, s, vbd_done, -2)
                        vb = vbd[:, s.slot(-1), :, :, :]
                        for c in range(NC_A):
                            if c == 4:
                                need(pe, s, pb_copied)
                            pe.matmul(ps_ao[:, 2 * c * VW:2 * (c + 1) * VW], probT[:, c * P:(c + 1) * P],
                                      vb[:, 0, 2 * c:2 * c + 2, :].rearrange("p h d -> p (h d)"),
                                      start=(c == 0), stop=False)
                        need(pe, s, pc_copied)
                        for c in range(NC_B):
                            last = pe.matmul(ps_ao[:, c * HPC * VW:(c + 1) * HPC * VW],
                                             probT[0:RB, 1024 + c * P:1024 + (c + 1) * P],
                                             vb[0:RB, 1, c * HPC:(c + 1) * HPC, :].rearrange("p h d -> p (h d)"),
                                             start=False, stop=(c == NC_B - 1))
                        last.then_inc(pv_done, 1)
                    if s.has(-2) or s.has(-6):
                        need(pe, s, pc_copied)
                        need(pe, s, pb_copied)
                        need(pe, s, xt_copied, -1)
                        need(pe, s, wo_taken)
                        if s.has(-2):
                            last = pe.matmul(ps_bw[:, 0:D], probT[:, 1280:1408], wo_s[:, :], start=True, stop=True)
                        if s.has(-5):
                            last = pe.matmul(ps_bw[:, D:D + E], xt[:, 1 - s.par(0), P:2 * P], wg_s[:, :], start=True, stop=True)
                        if s.has(-6):
                            need(pe, s, pick_done)
                            for col, lhs in ((D + E, ustri), (D + 2 * E, ones_b)):
                                for k in range(TOPK):
                                    last = pe.matmul(ps_bw[:, col:col + E], lhs[:, :], pick[:, s.par(-6), k, :],
                                                     start=(k == 0), stop=(k == TOPK - 1))
                        last.then_inc(wo_done, 1)
                run(pe, attend, step)

            @block.vector
            def _(dve):
                for t in (ps_ao, ps_bw, ps_c, ps_t):
                    last = dve.memset(t[:, :], 0.0)
                dve.wait_ge(s_mask, 16)
                dve.tensor_scalar(out=mask_b[:, :, :].rearrange("p b m -> p (b m)"), in0=mask_u8[:, :],
                                  scalar1=-1.0, scalar2=MASKED, op0=ALU.add, op1=ALU.mult).then_inc(const_dve, 1)
                dve.memset(mv[:, :, :, :], 1.0).then_inc(const_dve, 1)
                dve.wait_ge(const_pool, 10)
                dve.tensor_reduce(out=khead[:, :], in_=band[:, :].rearrange("p (g h) -> p h g", h=HPG), axis=AX_X,
                                  op=ALU.add).then_inc(const_dve, 1)
                dve.wait_ge(const_dve, 3)
                dve.tensor_scalar(out=khead[:, :], in0=khead[:, :], scalar1=SCALE, scalar2=None, op0=ALU.mult).then_inc(const_dve, 1)
                dve.wait_ge(const_dve, 4)
                dve.wait_ge(const_act, 1)
                dve.wait_ge(s_x[0], 16)

                def step(s):
                    if s.has(-2):
                        need(dve, s, pv_done, -1)
                        o = ps_ao[:, 0:HEADS * VW].rearrange("p (h d) -> p h d", d=VW)
                        dve.reciprocal(out=rden[:, s.par(0), :], in_=o[:, :, HD]).then_inc(rden_done, 1)
                        need(dve, s, rden_done)
                        dve.tensor_tensor(out=onorm[:, s.par(-2), :, :], in0=o[:, :, 0:HD],
                                          in1=rden[:, s.par(0), :].unsqueeze(2).to_broadcast([P, HEADS, HD]),
                                          op=ALU.mult).then_inc(onorm_done, 1)
                    if s.has(4):
                        dve.bn_stats(out=bnst[:, s.par(0), 0, :], in_=rows(x_all, s, 4)).then_inc(bn1_done, 1)
                    if s.has(-3):
                        need(dve, s, wo_done, -1)
                        dve.scalar_tensor_tensor(out=rows(x_all, s, -3), in0=ps_bw[:, 0:D], scalar=gains[:, 0:1],
                                                 in1=rows(x_all, s, -3), op0=ALU.mult, op1=ALU.add).then_inc(x1_done, 1)
                    if s.has(-8):
                        need(dve, s, prow_done, -1)
                        if s.looped or s.has(-10):
                            dve.wait_ge(scat[s.slot(-10)], (s.turn(-10) + 1) * (TOPK * 16))
                        with nc.allow_low_precision(reason="one term is not zero, a whole number below 2 ** 24"):
                            dve.tensor_reduce(out=dest[:, s.par(-8), :], in_=prow[:, s.par(-8), :, :], axis=AX_X,
                                              op=ALU.add).then_inc(dest_done, 1)
                    need(dve, s, wo_done, -1)
                    need(dve, s, next_done, -2)
                    need(dve, s, x1_done)
                    dve.tensor_copy(out=lrt[:, s.par(0), :, :].rearrange("p a e -> p (a e)"), in_=ps_bw[:, D:D + 3 * E]).then_inc(wo_taken, 1)
                    if s.has(-3):
                        dve.bn_stats(out=bnst[:, s.par(0), 1, :], in_=rows(x_all, s, -3)).then_inc(bn2_done, 1)
                    if s.has(3):
                        need(dve, s, rstd_done, -1)
                        need(dve, s, xt_done, -2)
                        need(dve, s, bn1_done)
                        need(dve, s, bn2_done)
                        k = s.slot(-1)
                        dve.tensor_scalar(out=xn1[:, s.par(3), :], in0=rows(x_all, s, 3), scalar1=mv[:, k, 0, 0:1],
                                          scalar2=rstd[:, k, 0:1], op0=ALU.subtract, op1=ALU.mult).then_inc(xn1_done, 1)
                    if s.has(-4):
                        need(dve, s, rstd_done, -1)
                        need(dve, s, wo_taken)
                        need(dve, s, m8_kept, -2)
                        need(dve, s, bn1_done)
                        need(dve, s, bn2_done)
                        k = s.slot(-1)
                        dve.tensor_scalar(out=xn2[:, s.par(-4), :], in0=rows(x_all, s, -4), scalar1=mv[:, k, 1, 0:1],
                                          scalar2=rstd[:, k, 1:2], op0=ALU.subtract, op1=ALU.mult).then_inc(xn2_done, 1)
                    if s.has(-6):
                        if not s.has(-4):
                            need(dve, s, wo_taken)
                            need(dve, s, m8_kept, -2)
                        dve.max(out=m8[:, s.par(-6), :], in_=lrt[:, s.par(0), 0, :]).then_inc(max8_done, 1)
                        need(dve, s, max8_done)
                        need(dve, s, pick_done, -2)
                        if s.looped or s.has(-10):
                            dve.wait_ge(scat[s.slot(-6)], (s.turn(-10) + 1) * (TOPK * 16))
                        k = s.slot(-3)
                        for c in range(TOPK):
                            last = dve.tensor_scalar(out=pay[:, s.slot(-6), c, 0:D], in0=rows(x_all, s, -6), scalar1=mv[:, k, 1, 0:1],
                                                     scalar2=rstd[:, k, 1:2], op0=ALU.subtract, op1=ALU.mult)
                        last.then_inc(pay_done, 1)
                        dve.max_index(out=ix8[:, s.par(-6), :], in_max=m8[:, s.par(-6), :], in_values=lrt[:, s.par(0), 0, :]).then_inc(ix8_done, 1)
                        need(dve, s, ix8_done)
                        need(dve, s, prow_done, -1)
                        dve.tensor_tensor(out=pick[:, s.par(-6), :, :], in0=iota_e[:, :, :],
                                          in1=ix8[:, s.par(-6), 0:TOPK].unsqueeze(2).to_broadcast([P, TOPK, E]),
                                          op=ALU.is_equal).then_inc(pick_done, 1)
                    if s.has(4) or s.has(-3):
                        if not s.has(3) or not s.has(-4):
                            need(dve, s, bn1_done)
                            need(dve, s, bn2_done)
                        if s.has(4):
                            last = dve.bn_aggr(out=mv[:, s.slot(0), 0, :], in_=bnst[:, s.par(0), 0, :])
                        if s.has(-3):
                            last = dve.bn_aggr(out=mv[:, s.slot(0), 1, :], in_=bnst[:, s.par(0), 1, :])
                        last.then_inc(mv_done, 1)
                    if s.has(0):
                        sc = ps_s[:, :, 0:SW].rearrange("p g (h m) -> p g h m", m=M)
                        need(dve, s, sc_done)
                        dve.tensor_reduce(out=smax[:, s.par(0), :].rearrange("p (g h) -> p g h", g=GROUPS), in_=sc, axis=AX_X,
                                          op=ALU.max).then_inc(max_done, 1)
                        need(dve, s, max_done)
                        need(dve, s, pc_done, -1)
                        for lo, hi in ((0, KA), (KA, M)):
                            part = prob[:, s.par(0), HEADS * lo:HEADS * hi].rearrange("p (g h m) -> p g h m", g=GROUPS, h=HPG)
                            top = smax[:, s.par(0), :].rearrange("p (g h) -> p g h", g=GROUPS).unsqueeze(3)
                            last = dve.tensor_tensor(out=part, in0=sc[:, :, :, lo:hi],
                                                     in1=top.to_broadcast([P, GROUPS, HPG, hi - lo]), op=ALU.subtract)
                        last.then_inc(sub_done, 1)


                def all_x():
                    for k in range(1, 4):
                        dve.wait_ge(s_x[k], 16)
                run(dve, attend, step, all_x)


        with ExitStack() as ps_es:
            def pb2(name, shape, dt=F32):
                return ps_es.enter_context(nc.psum_tensor(name, shape, dt))
            ps_x = pb2("ps_x", [P, 2, 512])
            ps_h = pb2("ps_h", [P, 2, 512])
            ps_f = pb2("ps_f", [P, 2, 512])
            ps_y = pb2("ps_y", [P, 2, 512])
            block = ps_es.enter_context(nc.Block())
            TAB_TAIL, TAB_GATES, TAB_TILES = 1, 12, 13

            @block.sync
            def _(sp):
                sp.wait_ge(s_tab, TAB_TAIL)
                for e in range(E):
                    row = sp.value_load(eint[0:1, 0, e:e + 1], min_val=e * SLOTS, max_val=e * SLOTS + NTOK)
                    sp.dma_start(expert_in[bass.ds(row, P), :], padrow[:, :]).then_inc(s_tail, 16)
                sp.wait_ge(s_tail, (TILES_PAD + E) * 16)
                sp.wait_ge(s_tab, TAB_TILES)

                def step(s):
                    if s.has(3):
                        col = tile_i[0:1, 1, bass.ds(s.n(3), 1)] if s.looped else tile_i[0:1, 1, s.n(3):s.n(4)]
                        row = sp.value_load(col, min_val=0, max_val=E * SLOTS + (TILES_PAD - 1) * P)
                        need(sp, s, to_done, -2)
                        sp.dma_start(xe[:, s.slot(3, 8), :], expert_in[bass.ds(row, P), :]).then_inc(xe_in[s.slot(3, 8)], 16)
                run(sp, experts, step)

            @block.gpsimd
            def _(pool):
                def step(s):
                    if s.has(-3) or s.has(-4):
                        need(pool, s, to_done, -1)
                    if s.has(-3):
                        need(pool, s, y_copied)
                        pool.tensor_tensor(out=to[:, s.slot(-3), :], in0=xe[:, s.slot(-3, 8), D:D + 1].bitcast(U32), in1=no_row[:, :],
                                           op=ALU.add).then_inc(to_done, 1)
                    if s.has(-4):
                        pool.indirect_dma_start(out=expert_out[:, :], out_offset=bass.IndirectOffsetOnAxis(ap=to[:, s.slot(-4), :], axis=0),
                                                in_=ye[:, s.slot(-4), :], in_offset=None, bounds_check=TOPK * NTOK - 1,
                                                oob_is_err=False).then_inc(y_out[s.slot(-4)], 16)
                run(pool, experts, step)
                for r in range(4):
                    pool.wait_ge(y_out[r], TILES // 4 * 16)

            @block.scalar
            def _(act):
                act.wait_ge(s_tab, TAB_GATES)
                act.activation(gate_d[:, :, :], gate_d[:, :, :], ACT.Exp).then_inc(s_gate, 1)

                def step(s):
                    if s.has(0):
                        need(act, s, h_done)
                        need(act, s, f_done, -2)
                        act.activation(sg[:, s.par(0), :], ps_h[:, s.par(0), 0:I], ACT.Silu).then_inc(silu_done, 1)
                    if s.has(-2):
                        need(act, s, ft_done)
                        act.activation(ffT[:, s.par(0), :], ps_f[:, s.par(0), 0:I], ACT.Copy).then_inc(ft_copied, 1)
                    if s.has(2):
                        need(act, s, xe_done)
                        act.activation(xeT[:, s.par(0), :], ps_x[:, s.par(0), 0:P], ACT.Copy).then_inc(xe_copied, 1)
                run(act, experts, step)

            @block.tensor
            def _(pe):
                pe.wait_ge(s_tab, TAB_TILES)
                pe.wait_ge(s_wffn, (2 + E) * 16)

                def step(s):
                    if s.has(0):
                        col = tile_i[0:1, 0, bass.ds(s.n(0), 1)] if s.looped else tile_i[0:1, 0, s.n(0):s.n(1)]
                        e = pe.value_load(col, min_val=0, max_val=E - 1)
                        need(pe, s, xe_copied, -2)
                        need(pe, s, f_done, -2)
                        pe.matmul(ps_h[:, s.par(0), :], xeT[:, s.par(0), :],
                                  w1_s[:, bass.ds(e, 1), :].rearrange("p a n -> p (a n)"), start=True, stop=True).then_inc(h_done, 1)
                    if s.has(-2):
                        need(pe, s, f_done, -2)
                        need(pe, s, ft_copied, -2)
                        for c in range(IC):
                            last = pe.transpose(ps_f[:, s.par(0), c * P:(c + 1) * P], ff[:, s.slot(-2), c * P:(c + 1) * P], ident[:, :])
                        last.then_inc(ft_done, 1)
                    if s.has(2):
                        pe.wait_ge(xe_in[s.slot(2, 8)], (s.turn(2, 8) + 1) * 16)
                        need(pe, s, xe_copied, -2)
                        pe.transpose(ps_x[:, s.par(0), 0:P], xe[:, s.slot(2, 8), 0:D], ident[:, :]).then_inc(xe_done, 1)
                    if s.has(-3):
                        col = tile_i[0:1, 0, bass.ds(s.n(-3), 1)] if s.looped else tile_i[0:1, 0, s.n(-3):s.n(-2)]
                        e = pe.value_load(col, min_val=0, max_val=E - 1)
                        need(pe, s, ft_copied, -1)
                        need(pe, s, y_copied, -2)
                        for c in range(IC):
                            last = pe.matmul(ps_y[:, s.par(0), 0:D], ffT[:, s.par(-3), c * P:(c + 1) * P],
                                             w2_s[:, bass.ds(e, 1), c, :].rearrange("p a n -> p (a n)"), start=(c == 0), stop=(c == IC - 1))
                        last.then_inc(y_done, 1)
                run(pe, experts, step)

            @block.vector
            def _(dve):
                links = [0]

                def link(ins):
                    links[0] += 1
                    ins.then_inc(s_tab, 1)
                    dve.wait_ge(s_tab, links[0])

                dve.wait_ge(s_pad, 6)
                link(dve.tensor_copy(out=eint[:, 0, :], in_=nextrow[:, :]))
                link(dve.tensor_tensor(out=etab[:, 0, :], in0=nextrow[:, :], in1=eoff[:, :], op=ALU.subtract))
                link(dve.tensor_scalar(out=eint[:, 1, :], in0=etab[:, 0, :], scalar1=float(P - 1), scalar2=None, op0=ALU.add))
                link(dve.tensor_scalar(out=eint[:, 2, :], in0=eint[:, 1, :], scalar1=7, scalar2=None, op0=ALU.arith_shift_right))
                link(dve.tensor_copy(out=etab[:, 1, :], in_=eint[:, 2, :]))
                n_j = etab[:, 1, :].unsqueeze(1).to_broadcast([P, E, E])
                link(dve.tensor_tensor(out=past[:, 0:E, :], in0=n_j, in1=lower[:, :, :], op=ALU.mult))
                link(dve.tensor_reduce(out=etab[:, 2, :], in_=past[:, 0:E, :], axis=AX_X, op=ALU.add))
                link(dve.tensor_scalar(out=etab[:, 3, :], in0=etab[:, 1, :], scalar1=-float(P), scalar2=float(SLOTS), op0=ALU.mult, op1=ALU.add))
                link(dve.tensor_tensor(out=past[:, :, :], in0=iota_t[:, :].unsqueeze(2).to_broadcast([P, TILES, E]),
                                       in1=etab[:, 2, :].unsqueeze(1).to_broadcast([P, TILES, E]), op=ALU.is_ge))
                with nc.allow_low_precision(reason="whole numbers below 2 ** 24"):
                    dve.tensor_reduce(out=tile_f[:, 0, :], in_=past[:, :, :], axis=AX_X, op=ALU.add)
                    link(dve.tensor_tensor(out=pastr[:, :, :], in0=past[:, :, :],
                                           in1=etab[:, 3, :].unsqueeze(1).to_broadcast([P, TILES, E]), op=ALU.mult))
                    dve.tensor_scalar(out=tile_i[:, 0, :], in0=tile_f[:, 0, :], scalar1=float(E - 1), scalar2=None, op0=ALU.min)
                    link(dve.tensor_reduce(out=tile_f[:, 1, :], in_=pastr[:, :, :], axis=AX_X, op=ALU.add))
                    link(dve.tensor_tensor(out=gate_d[:, :, :], in0=m8_all[:, :, :],
                                           in1=m8_all[:, :, 0:1].to_broadcast([P, NB, E]), op=ALU.subtract))
                raise_tiles = dve.scalar_tensor_tensor(out=tile_i[:, 1, :], in0=iota_t[:, :], scalar=float(P), in1=tile_f[:, 1, :],
                                                       op0=ALU.mult, op1=ALU.add)
                link(raise_tiles)

                def gates():
                    dve.wait_ge(s_gate, 1)
                    link(dve.tensor_reduce(out=gate_s[:, 0, :], in_=gate_d[:, :, :], axis=AX_X, op=ALU.add))
                    link(dve.tensor_tensor(out=gate_s[:, 1, :], in0=gate_d[:, :, 0], in1=gate_d[:, :, 1], op=ALU.add))
                    link(dve.scalar_tensor_tensor(out=gate_s[:, 2, :], in0=gate_s[:, 0, :], scalar=GATE_EPS, in1=gate_s[:, 1, :],
                                                  op0=ALU.mult, op1=ALU.add))
                    link(dve.reciprocal(out=gate_s[:, 0, :], in_=gate_s[:, 2, :]))
                    for k in range(TOPK):
                        link(dve.scalar_tensor_tensor(out=gate_w[:, k, :], in0=gate_d[:, :, k], scalar=gains[:, 1:2], in1=gate_s[:, 0, :],
                                                      op0=ALU.mult, op1=ALU.mult))

                def step(s):
                    if s.has(0):
                        need(dve, s, silu_done)
                        need(dve, s, ft_done, -2)
                        dve.tensor_tensor(out=ff[:, s.slot(0), :], in0=sg[:, s.par(0), :], in1=ps_h[:, s.par(0), I:2 * I],
                                          op=ALU.mult).then_inc(f_done, 1)
                    if s.has(-3):
                        if s.looped or s.has(-7):
                            dve.wait_ge(y_out[s.slot(-3)], (s.turn(-7) + 1) * 16)
                        need(dve, s, y_done)
                        dve.tensor_copy(out=ye[:, s.slot(-3), :], in_=ps_y[:, s.par(0), 0:D]).then_inc(y_copied, 1)
                gates()
                run(dve, experts, step)

        NCH = NB // CB
        with nc.Block() as block:
            def chunk(t, j):
                return t[:, bass.ds(j * CB, CB), :]

            @block.sync
            def _(sp):
                def load(j, c):
                    for k in range(TOPK):
                        src = expert_out[bass.ds(j * (CB * T) + k * NTOK, CB * T), :].rearrange("(b t) d -> t b d", t=T)
                        sp.dma_start(yk[:, c, k, :, :], src).then_inc(s_y[c], 16)
                for c in range(2):
                    load(c, c)
                with sp.Fori(0, NCH // 2 - 1) as j:
                    for c in range(2):
                        sp.wait_ge(s_sum, j * (2 * CB) + (c + 1) * CB)
                        load(j * 2 + (2 + c), c)

            @block.scalar
            def _(act):
                with act.Fori(0, NCH) as j:
                    act.wait_ge(s_sum, (j + 1) * CB)
                    act.dma_start(out[bass.ds(j * CB, CB), :, :].rearrange("b t d -> t b d"), chunk(x_all, j)).then_inc(s_out, 16)
                act.wait_ge(s_out, NCH * 16)

            @block.vector
            def _(dve):
                with dve.Fori(0, NCH // 2) as j:
                    for c in range(2):
                        dve.wait_ge(s_y[c], (j + 1) * (TOPK * 16))
                        for b in range(CB):
                            i = j * (2 * CB) + (c * CB + b)
                            xb = x_all[:, bass.ds(i, 1), :].rearrange("p a d -> p (a d)")
                            y0, y1 = yk[:, c, 0, b, :], yk[:, c, 1, b, :]
                            dve.scalar_tensor_tensor(out=y0, in0=y0, scalar=gate_w[:, 0, bass.ds(i, 1)], in1=xb,
                                                     op0=ALU.mult, op1=ALU.add).then_inc(s_half_sum, 1)
                            dve.wait_ge(s_half_sum, j * (2 * CB) + (c * CB + b + 1))
                            dve.scalar_tensor_tensor(out=xb, in0=y1, scalar=gate_w[:, 1, bass.ds(i, 1)], in1=y0,
                                                     op0=ALU.mult, op1=ALU.add).then_inc(s_sum, 1)


_INS = ['x', 'ctx_768', 'mask_BxS2_bf1', 'g_xattn', 'g_ffn', 'L0_xattn_Wq', 'L0_xattn_Wk', 'L0_xattn_Wv', 'L0_xattn_Wo',
        'L0_ffn_Wg', 'L0_ffn_W11', 'L0_ffn_W12', 'L0_ffn_W2']


def kernel(**inputs):
    import numpy as np
    import concourse.bacc as bacc
    from concourse.bass_utils import run_bass_kernel_spmd

    nc = bacc.Bacc("TRN2", target_bir_lowering=False, num_devices=1)
    arrays, args = {}, []
    for name in _INS:
        a = np.ascontiguousarray(inputs[name])
        if a.dtype == np.bool_:
            a = a.view(np.uint8)
        if name == "ctx_768":
            a = a.transpose(0, 2, 1)
            rest = [a[:, :, KA:]] * 8
            pad = np.zeros(a.shape[:2] + (2 * P - 2 * KA - sum(r.shape[2] for r in rest),), a.dtype)
            a = np.ascontiguousarray(np.concatenate([a[:, :, :KA], a[:, :, :KA], *rest, pad], axis=2))
        arrays[f"in_{name}"] = a
        args.append(nc.dram_tensor(f"in_{name}", a.shape, mybir.dt.from_np(a.dtype), kind="ExternalInput").ap())
    shape = arrays["in_x"].shape
    args.append(nc.dram_tensor("out", shape, F32, kind="ExternalOutput").ap())
    flamingo_block(nc, *args)
    r = run_bass_kernel_spmd(nc, [arrays], core_ids=[0])
    return r.results[0]["out"]
```

```python
from contextlib import ExitStack

import concourse.bass as bass
from concourse import mybir

P = 128
ALU = mybir.AluOpType
ACT = mybir.ActivationFunctionType
F32 = mybir.dt.float32
BF16 = mybir.dt.bfloat16
U8 = mybir.dt.uint8
AX_X = mybir.AxisListType.X

HEADS = 16
TOPK = 2
U32 = mybir.dt.uint32
I32 = mybir.dt.int32
HD = 8
GROUPS = 4
HPG = HEADS // GROUPS
KA = 64
UNROLL = 4
LN_EPS = 1e-5
GATE_EPS = 1e-8
MASKED = 3.3895313892515355e38


def flamingo_block(nc, x, ctx_in, mask, g_xattn, g_ffn, wq, wk, wv, wo, wg, w11, w12, w2, out):
    NB, T, D = x.shape
    C = ctx_in.shape[1]
    M = mask.shape[1]
    E, _, I = w11.shape
    KB = M - KA
    HPC = 8
    RB = HPC * KB
    NC_A = HEADS // 2
    NC_B = HEADS // HPC
    SW = HPG * M
    VW = HD + 1
    IC = I // P
    NTOK = NB * T
    TILES_PAD = E
    TILES = TOPK * NTOK // P + E
    SCALE = float(HD) ** -0.5
    assert T == P and D == P and HEADS * HD == D and RB <= P and SW <= 512

    with ExitStack() as es:
        def sb(name, shape, dt=F32):
            return es.enter_context(nc.sbuf_tensor(name, shape, dt))

        def sem(name):
            return es.enter_context(nc.semaphore(name))

        x_all = sb("x_all", [P, NB, D])
        m8_all = sb("m8_all", [P, NB, E])
        wq_s = sb("wq_s", [P, D])
        wk_s = sb("wk_s", [P, D])
        wv_s = sb("wv_s", [P, D])
        wo_s = sb("wo_s", [P, D])
        wg_s = sb("wg_s", [P, E])
        w1_s = sb("w1_s", [P, E, 2 * I])
        w2_s = sb("w2_s", [P, E, IC, D])
        gains = sb("gains", [P, 2])
        ident = sb("ident", [P, P])
        SLOTS = NTOK + P
        ROW = D + 4
        expert_in = nc.dram_tensor("expert_in", [E * SLOTS + TILES_PAD * P, ROW], F32, kind="Internal")
        expert_out = nc.dram_tensor("expert_out", [TOPK * NTOK, D], F32, kind="Internal")
        pay = sb("pay", [P, UNROLL, TOPK, ROW])

        PADDING = 1 << 20
        padrow = sb("padrow", [P, ROW])
        eoff = sb("eoff", [P, E])
        etab = sb("etab", [P, 8, E])
        eint = sb("eint", [P, 3, E], I32)
        lower = sb("lower", [P, E, E])
        iota_t = sb("iota_t", [P, TILES])
        past = sb("past", [P, TILES, E])
        pastr = sb("pastr", [P, TILES, E])
        tile_f = sb("tile_f", [P, 3, TILES])
        tile_i = sb("tile_i", [P, 2, TILES], I32)
        gate_d = sb("gate_d", [P, NB, E])
        gate_s = sb("gate_s", [P, 3, NB])
        gate_w = sb("gate_w", [P, TOPK, NB])
        xe = sb("xe", [P, 8, ROW])
        xeT = sb("xeT", [P, 4, P])
        sg = sb("sg", [P, 2, I])
        w1e = sb("w1e", [P, 2, 2 * I])
        ff = sb("ff", [P, 4, I])
        ye = sb("ye", [P, 4, D])
        to = sb("to", [P, 4, 1], U32)
        no_row = sb("no_row", [P, 1], U32)
        YR = 4
        CB = 4
        yk = sb("yk", [P, YR, TOPK, CB, D])

        mask_u8 = sb("mask_u8", [P, NB * M], U8)
        mask_b = sb("mask_b", [P, NB, M], BF16)
        ones_b = sb("ones_b", [P, P], BF16)
        band = sb("band", [P, HEADS])
        khead = sb("khead", [P, HEADS])
        vhead = sb("vhead", [P, 2, HEADS])
        neg_half = sb("neg_half", [P, 2])
        eps = sb("eps", [P, 2])
        ctxT = sb("ctxT", [C, UNROLL, 2 * P])
        xn1 = sb("xn1", [P, 2, D])
        xn2 = sb("xn2", [P, 2, D])
        xt = sb("xt", [P, 2, 2 * P])
        vkq = sb("vkq", [P, 2, 2 * D + M + P])
        kbd = sb("kbd", [P, 2, HEADS, M])
        vbd = sb("vbd", [P, UNROLL, 2, HEADS, VW])
        prob = sb("prob", [P, 2, HEADS * M])
        smax = sb("smax", [P, 2, HEADS])
        probT = sb("probT", [P, 8 * P + 2 * P + P])
        rden = sb("rden", [P, 2, HEADS])
        onorm = sb("onorm", [P, 2, HEADS, HD])
        bnst = sb("bnst", [P, 2, 2, 6])
        mv = sb("mv", [P, UNROLL, 2, 2])
        vare = sb("vare", [P, UNROLL, 2])
        rstd = sb("rstd", [P, UNROLL, 2])
        lrt = sb("lrt", [P, 2, 3, E])
        m8 = sb("m8", [P, 2, E])
        ix8 = sb("ix8", [P, 2, E], U32)
        pick = sb("pick", [P, 2, TOPK, E], BF16)
        iota_e = sb("iota_e", [P, TOPK, E])
        nextrow = sb("nextrow", [P, E])
        row8 = sb("row8", [P, 2, E])
        prow = sb("prow", [P, 2, TOPK, E])
        dest = sb("dest", [P, 2, TOPK], U32)
        ustri = sb("ustri", [P, P], BF16)
        turn_add = sb("turn_add", [P, TOPK], U32)

        s_x = [sem(f"s_x{i}") for i in range(6)]
        s_w = sem("s_w")
        s_wffn = sem("s_wffn")
        s_mask = sem("s_mask")
        s_ctx = [sem(f"s_ctx{i}") for i in range(UNROLL)]
        s_g = sem("s_g")
        const_pool = sem("const_pool")
        const_dve = sem("const_dve")
        const_act = sem("const_act")
        sc_done = sem("sc_done")
        sub_done = sem("sub_done")
        max_done = sem("max_done")
        exp_done = sem("exp_done")
        vkq_done = sem("vkq_done")
        vkq_copied = sem("vkq_copied")
        pa_done = sem("pa_done")
        pb_done = sem("pb_done")
        pc_done = sem("pc_done")
        pa_copied = sem("pa_copied")
        pb_copied = sem("pb_copied")
        pc_copied = sem("pc_copied")
        xt_done = sem("xt_done")
        xt_copied = sem("xt_copied")
        pv_done = sem("pv_done")
        wo_done = sem("wo_done")
        rden_done = sem("rden_done")
        onorm_done = sem("onorm_done")
        wo_taken = sem("wo_taken")
        x1_done = sem("x1_done")
        m8_kept = sem("m8_kept")
        max8_done = sem("max8_done")
        ix8_done = sem("ix8_done")
        pick_done = sem("pick_done")
        row8_done = sem("row8_done")
        prow_done = sem("prow_done")
        next_done = sem("next_done")
        dest_done = sem("dest_done")
        pay_done = sem("pay_done")
        tok_done = sem("tok_done")
        scat = [sem(f"scat{i}") for i in range(UNROLL)]
        s_pad = sem("s_pad")
        s_tail = sem("s_tail")
        s_tab = sem("s_tab")
        s_gate = sem("s_gate")
        xe_in = [sem(f"xe_in{i}") for i in range(8)]
        xe_done = sem("xe_done")
        xe_copied = sem("xe_copied")
        h_done = sem("h_done")
        silu_done = sem("silu_done")
        f_done = sem("f_done")
        w1_copied = sem("w1_copied")
        y_done = sem("y_done")
        y_copied = sem("y_copied")
        to_done = sem("to_done")
        y_out = [sem(f"y_out{i}") for i in range(4)]
        s_y = [sem(f"s_y{i}") for i in range(YR)]
        s_sum = sem("s_sum")
        s_out = sem("s_out")
        s_half_sum = sem("s_half_sum")
        bn1_done = sem("bn1_done")
        bn2_done = sem("bn2_done")
        mv_done = sem("mv_done")
        var_done = sem("var_done")
        rstd_done = sem("rstd_done")
        xn1_done = sem("xn1_done")
        xn2_done = sem("xn2_done")
        kbd_done = sem("kbd_done")
        kbd2_done = sem("kbd2_done")
        vbd_done = sem("vbd_done")

        class Plan:
            def __init__(self, total, unroll, first, loop0, loop1, last):
                assert first % unroll == 0 and loop0 % unroll == 0 and loop1 % unroll == 0
                self.total, self.unroll, self.first, self.loop0, self.loop1, self.last = total, unroll, first, loop0, loop1, last

        class Step:
            def __init__(self, plan, j, off, looped):
                self.plan, self.j, self.off, self.looped = plan, j, off, looped

            def has(self, lag):
                return self.looped or 0 <= self.plan.unroll * self.j + self.off + lag < self.plan.total

            def n(self, k):
                return self.j * self.plan.unroll + (self.off + k)

            def par(self, lag):
                return (self.off + lag) % 2

            def slot(self, lag, ring=4):
                return (self.off + lag) % ring

            def turn(self, lag, ring=4):
                return self.j * (self.plan.unroll // ring) + (self.off + lag) // ring

        def run(eng, plan, step, before_loop=lambda: None, turn=lambda j, looped: None):
            u = plan.unroll
            for s in range(plan.first, plan.loop0):
                if s % u == 0:
                    turn(s // u, False)
                step(Step(plan, s // u, s % u, False))
            before_loop()
            with eng.Fori(plan.loop0 // u, plan.loop1 // u) as j:
                turn(j, True)
                for off in range(u):
                    step(Step(plan, j, off, True))
            for s in range(plan.loop1, plan.last + 1):
                if s % u == 0:
                    turn(s // u, False)
                step(Step(plan, s // u, s % u, False))

        FIRST, LOOP0 = -UNROLL, 3 * UNROLL
        attend = Plan(NB, UNROLL, FIRST, LOOP0, NB - 2 * UNROLL, NB + 7)
        experts = Plan(TILES, 8, -8, 8, TILES - 8, TILES + 2)

        LAGS = {
            sc_done: (0,), max_done: (0,), sub_done: (0,), exp_done: (-1,), vkq_done: (2,), vkq_copied: (2,),
            pa_done: (-1,), pb_done: (-1,), pc_done: (-1, -2), pa_copied: (-1,), pb_copied: (-1,), pc_copied: (-1, -2),
            xt_done: (3, -4), xt_copied: (3, -4), pv_done: (-1,), wo_done: (-2, -6), rden_done: (-2,), onorm_done: (-2,),
            x1_done: (-3,), wo_taken: (4, -7), bn1_done: (4,), bn2_done: (-3,), mv_done: (4, -3), var_done: (4, -3),
            rstd_done: (4, -3), xn1_done: (3,), xn2_done: (-4,), pay_done: (-6,), max8_done: (-6,), ix8_done: (-6,),
            m8_kept: (-6,), pick_done: (-6,), row8_done: (-7,), prow_done: (-7,), next_done: (-7,), dest_done: (-8,),
            tok_done: (-8,), kbd_done: (2,), kbd2_done: (2,), vbd_done: (1,),
            xe_done: (2,), xe_copied: (2,), h_done: (0,), silu_done: (0,), f_done: (0,), w1_copied: (1,),
            y_done: (-2,), y_copied: (-2,), to_done: (-2,),
        }

        def need(eng, s, signal, step=0):
            first, last = max(LAGS[signal]), min(LAGS[signal])
            if s.looped:
                eng.wait_ge(signal, s.n(step + first + 1))
                return
            count = min(s.n(step) + first + 1, s.plan.total + first - last)
            if count > 0:
                eng.wait_ge(signal, count)

        def batch(t, s, lag):
            return t[:, bass.ds(s.n(lag), 1)] if s.looped else t[:, s.n(lag):s.n(lag) + 1]

        def rows(t, s, lag):
            return batch(t, s, lag).rearrange("p a d -> p (a d)")

        XC = [0, 2, 6, LOOP0 + 4, 29, 46, NB]
        XN = len(XC) - 1
        KBD_DVE = 8

        def spread_keys(eng, s, lo, hi):
            return eng.tensor_tensor(out=kbd[:, s.par(2), lo:hi, :],
                                     in0=vkq[:, s.par(2), 2 * D:2 * D + M].unsqueeze(1).to_broadcast([P, hi - lo, M]),
                                     in1=khead[:, lo:hi].unsqueeze(2).to_broadcast([P, hi - lo, M]), op=ALU.mult)

        with ExitStack() as ps_es:
            def pb(name, shape, dt=F32):
                return ps_es.enter_context(nc.psum_tensor(name, shape, dt))
            ps_s = pb("ps_s", [P, GROUPS, 512])
            ps_ao = pb("ps_ao", [P, 512])
            ps_bw = pb("ps_bw", [P, 512])
            ps_c = pb("ps_c", [P, 512])
            ps_t = pb("ps_t", [P, 512])
            block = ps_es.enter_context(nc.Block())

            @block.sync
            def _(sp):
                for k in range(XN):
                    sp.dma_start(x_all[:, XC[k]:XC[k + 1], :],
                                 x[XC[k]:XC[k + 1], :, :].rearrange("b t d -> t b d")).then_inc(s_x[k], 16)
                    if k == 0:
                        for dst, src in ((wk_s[0:C, :], wk), (wv_s[0:C, :], wv), (wq_s[:, :], wq),
                                         (wo_s[:, :], wo), (wg_s[:, :], wg)):
                            sp.dma_start(dst, src).then_inc(s_w, 16)
                sp.dma_start(w1_s[:, :, 0:I], w11.rearrange("e h i -> h e i")).then_inc(s_wffn, 16)
                sp.dma_start(w1_s[:, :, I:2 * I], w12.rearrange("e h i -> h e i")).then_inc(s_wffn, 16)
                for e in range(E):
                    sp.dma_start(w2_s[:, e, :, :], w2[e, :, :].rearrange("(c i) h -> i c h", c=IC)).then_inc(s_wffn, 16)
                sp.wait_ge(s_pad, 2)
                for k in range(TILES_PAD):
                    sp.dma_start(expert_in[E * SLOTS + k * P:E * SLOTS + (k + 1) * P, :], padrow[:, :]).then_inc(s_tail, 16)

            @block.gpsimd
            def _(pool):
                pool.memset(ident[:, :], 0.0).then_inc(const_pool, 1)
                pool.memset(band[:, :], 1.0).then_inc(const_pool, 1)
                pool.memset(vhead[:, :, :], 1.0).then_inc(const_pool, 1)
                pool.memset(ustri[:, :], 1.0).then_inc(const_pool, 1)
                pool.memset(ones_b[:, :], 1.0).then_inc(const_pool, 1)
                pool.memset(eps[:, :], LN_EPS)
                pool.memset(neg_half[:, :], -0.5).then_inc(const_pool, 1)
                pool.memset(vbd[:, :, :, :, :], 1.0).then_inc(const_pool, 1)
                pool.wait_ge(const_pool, 7)
                pool.affine_select(out=ident[:, :], in_=ident[:, :], compare_op=ALU.not_equal, fill=1.0,
                                   base=0, pattern=[[-1, P]], channel_multiplier=1).then_inc(const_pool, 1)
                pool.affine_select(out=band[:, :], in_=band[:, :], compare_op=ALU.is_ge, fill=0.0,
                                   base=0, pattern=[[-HD, HEADS]], channel_multiplier=1).then_inc(const_pool, 1)
                pool.wait_ge(const_pool, 9)
                pool.affine_select(out=band[:, :], in_=band[:, :], compare_op=ALU.is_ge, fill=0.0,
                                   base=HD - 1, pattern=[[HD, HEADS]], channel_multiplier=-1).then_inc(const_pool, 1)
                v = vhead[:, 0, :].rearrange("p (a b) -> p a b", b=2)
                pool.affine_select(out=v[:, :, 0:1], in_=v[:, :, 0:1], compare_op=ALU.is_ge, fill=0.0,
                                   base=KA - 1, pattern=[[0, HEADS // 2], [0, 1]], channel_multiplier=-1).then_inc(const_pool, 1)
                pool.affine_select(out=v[:, :, 1:2], in_=v[:, :, 1:2], compare_op=ALU.is_ge, fill=0.0,
                                   base=-KA, pattern=[[0, HEADS // 2], [0, 1]], channel_multiplier=1).then_inc(const_pool, 1)
                w = vhead[:, 1, :].rearrange("p (a b) -> p a b", b=HPC)
                pool.affine_select(out=w, in_=w, compare_op=ALU.is_ge, fill=0.0,
                                   base=0, pattern=[[0, NC_B], [-KB, HPC]], channel_multiplier=1).then_inc(const_pool, 1)
                pool.wait_ge(const_pool, 13)
                pool.affine_select(out=w, in_=w, compare_op=ALU.is_ge, fill=0.0,
                                   base=KB - 1, pattern=[[0, NC_B], [KB, HPC]], channel_multiplier=-1).then_inc(const_pool, 1)
                pool.wait_ge(const_pool, 14)
                for r in range(UNROLL):
                    pool.tensor_copy(out=vbd[:, r, :, :, HD], in_=vhead[:, :, :]).then_inc(const_pool, 1)

                pool.affine_select(out=ustri[:, :], in_=ustri[:, :], compare_op=ALU.is_ge, fill=0.0,
                                   base=-1, pattern=[[1, P]], channel_multiplier=-1).then_inc(const_pool, 1)
                pool.iota(iota_e[:, :, :], pattern=[[0, TOPK], [1, E]], base=0, channel_multiplier=0,
                          allow_small_or_imprecise_dtypes=True).then_inc(const_pool, 1)
                pool.iota(nextrow[:, :], pattern=[[SLOTS, E]], base=0, channel_multiplier=0,
                          allow_small_or_imprecise_dtypes=True).then_inc(const_pool, 1)
                pool.memset(turn_add[:, :], UNROLL * T).then_inc(const_pool, 1)
                pool.memset(padrow[:, 0:D], 0.0).then_inc(s_pad, 1)
                pool.memset(padrow[:, D:ROW].bitcast(U32), PADDING).then_inc(s_pad, 1)
                pool.iota(eoff[:, :], pattern=[[SLOTS, E]], base=0, channel_multiplier=0,
                          allow_small_or_imprecise_dtypes=True).then_inc(s_pad, 1)
                pool.iota(iota_t[:, :], pattern=[[1, TILES]], base=0, channel_multiplier=0,
                          allow_small_or_imprecise_dtypes=True).then_inc(s_pad, 1)
                pool.memset(lower[:, :, :], 1.0).then_inc(s_pad, 1)
                pool.memset(no_row[:, :], 0)
                pool.wait_ge(s_pad, 5)
                pool.affine_select(out=lower[:, :, :], in_=lower[:, :, :], compare_op=ALU.is_ge, fill=0.0,
                                   base=0, pattern=[[1, E], [-1, E]], channel_multiplier=0).then_inc(s_pad, 1)
                pool.memset(pay[:, :, :, :], 0.0).then_inc(const_pool, 1)
                pool.wait_ge(const_pool, 14 + UNROLL + 5)
                for r in range(UNROLL):
                    pool.iota(pay[:, r, :, D:D + 1].bitcast(I32), pattern=[[NTOK, TOPK]], base=(r - UNROLL) * T, channel_multiplier=1,
                              allow_small_or_imprecise_dtypes=True).then_inc(const_pool, 1)
                CONSTS = 14 + UNROLL + 5 + UNROLL
                pool.wait_ge(const_pool, CONSTS)
                pool.wait_ge(const_dve, 3)

                def step(s):
                    if s.has(4) or s.has(-3):
                        k = s.slot(0)
                        need(pool, s, mv_done)
                        pool.tensor_tensor(out=vare[:, k, :], in0=mv[:, k, :, 1], in1=eps[:, :], op=ALU.add).then_inc(var_done, 1)
                        need(pool, s, var_done)
                        pool.tensor_tensor(out=rstd[:, k, :], in0=vare[:, k, :], in1=neg_half[:, :],
                                           op=ALU.pow).then_inc(rstd_done, 1)
                    if s.has(-7):
                        k = s.par(-7)
                        need(pool, s, wo_taken)
                        need(pool, s, next_done, -1)
                        pool.tensor_tensor(out=row8[:, k, :], in0=lrt[:, s.par(0), 1, :], in1=nextrow[:, :], op=ALU.add).then_inc(row8_done, 1)
                        need(pool, s, row8_done)
                        pool.tensor_tensor(out=prow[:, k, :, :], in0=pick[:, k, :, :],
                                           in1=row8[:, k, :].unsqueeze(1).to_broadcast([P, TOPK, E]), op=ALU.mult).then_inc(prow_done, 1)
                        need(pool, s, prow_done)
                        pool.tensor_tensor(out=nextrow[:, :], in0=nextrow[:, :], in1=lrt[:, s.par(0), 2, :], op=ALU.add).then_inc(next_done, 1)
                    if s.has(-8):
                        need(pool, s, dest_done)
                        need(pool, s, pay_done, -2)
                        tok = pay[:, s.slot(-8), :, D:D + 1].bitcast(U32).rearrange("p k a -> p (k a)")
                        pool.tensor_tensor(out=tok, in0=tok, in1=turn_add[:, :], op=ALU.add).then_inc(tok_done, 1)
                    if s.has(-6):
                        need(pool, s, max8_done)
                        need(pool, s, tok_done)
                        pool.tensor_copy(out=rows(m8_all, s, -6), in_=m8[:, s.par(-6), :]).then_inc(m8_kept, 1)
                    if s.has(-8):
                        if not s.has(-6):
                            need(pool, s, tok_done)
                        for c in range(TOPK):
                            pool.indirect_dma_start(out=expert_in[:, :],
                                                    out_offset=bass.IndirectOffsetOnAxis(ap=dest[:, s.par(-8), c:c + 1], axis=0),
                                                    in_=pay[:, s.slot(-8), c, :], in_offset=None).then_inc(scat[s.slot(-8)], 16)
                    if s.has(1):
                        need(pool, s, vkq_copied, -1)
                        need(pool, s, pv_done, -2)
                        src = vkq[:, s.par(1), 0:2 * D].rearrange("p (c h d) -> p (c h) d", c=2, d=HD)
                        pool.tensor_tensor(out=vbd[:, s.slot(1), :, :, 0:HD].rearrange("p c h d -> p (c h) d"), in0=src,
                                           in1=vhead[:, :, :].rearrange("p c h -> p (c h)").unsqueeze(2).to_broadcast([P, 2 * HEADS, HD]),
                                           op=ALU.mult).then_inc(vbd_done, 1)
                    if s.has(2):
                        need(pool, s, sc_done)
                        need(pool, s, vkq_copied)
                        spread_keys(pool, s, KBD_DVE, HEADS).then_inc(kbd_done, 1)

                run(pool, attend, step)
                for r in range(UNROLL):
                    pool.wait_ge(scat[r], NB // UNROLL * TOPK * 16)

            @block.scalar
            def _(act):
                act.dma_start(mask_u8[:, :], mask.rearrange("b m -> (b m)").unsqueeze(0).to_broadcast([P, NB * M])).then_inc(s_mask, 16)
                act.dma_start(gains[:, 0:1], g_xattn.unsqueeze(0).to_broadcast([P, 1])).then_inc(s_g, 16)
                act.dma_start(gains[:, 1:2], g_ffn.unsqueeze(0).to_broadcast([P, 1])).then_inc(s_g, 16)

                def load_ctx(s, lag):
                    k = s.slot(lag)
                    src = ctx_in[bass.ds(s.n(lag), 1), :, :].rearrange("a c m -> (a c) m") if s.looped else ctx_in[s.n(lag), :, :]
                    act.dma_start(ctxT[:, k, :], src).then_inc(s_ctx[k], 16)

                for b in range(FIRST + 6):
                    load_ctx(Step(attend, 0, b, False), 0)
                act.wait_ge(s_g, 32)
                act.activation(gains[:, :], gains[:, :], ACT.Tanh).then_inc(const_act, 1)

                def step(s):
                    if s.has(-1):
                        need(act, s, sub_done, -1)
                        act.activation(prob[:, s.par(-1), :], prob[:, s.par(-1), :], ACT.Exp).then_inc(exp_done, 1)
                    if s.has(2):
                        need(act, s, vkq_done)
                        need(act, s, vbd_done, -1)
                        need(act, s, kbd_done, -2)
                        need(act, s, kbd2_done, -2)
                        act.activation(vkq[:, s.par(2), :], ps_t[:, 0:2 * D + M + P], ACT.Copy).then_inc(vkq_copied, 1)
                    if s.has(-1):
                        need(act, s, pa_done)
                        act.activation(probT[:, 0:512], ps_ao[:, :], ACT.Copy).then_inc(pa_copied, 1)
                        need(act, s, pb_done)
                        act.activation(probT[:, 512:1024], ps_bw[:, :], ACT.Copy).then_inc(pb_copied, 1)
                    if s.has(-1) or s.has(-2):
                        need(act, s, pc_done)
                        act.activation(probT[:, 1024:1408], ps_c[:, 0:384], ACT.Copy).then_inc(pc_copied, 1)
                    if s.has(3) or s.has(-4):
                        need(act, s, xt_done)
                        act.activation(xt[:, s.par(0), :], ps_t[:, 0:2 * P], ACT.Copy).then_inc(xt_copied, 1)
                    if s.has(6):
                        need(act, s, vkq_done)
                        load_ctx(s, 6)
                run(act, attend, step)

            @block.tensor
            def _(pe):
                pe.wait_ge(const_pool, 14 + UNROLL + 5)
                pe.wait_ge(s_w, 5 * 16)
                pe.wait_ge(const_dve, 1)

                def step(s):
                    if s.has(0):
                        k = s.par(0)
                        need(pe, s, vkq_copied, -2)
                        need(pe, s, kbd_done, -2)
                        need(pe, s, kbd2_done, -2)
                        need(pe, s, sub_done, -1)
                        bias = mask_b[0:1, bass.ds(s.n(0), 1), :] if s.looped else mask_b[0:1, s.n(0):s.n(1), :]
                        for g in range(GROUPS):
                            pe.matmul(ps_s[:, g, 0:SW], vkq[:, k, 2 * D + M:],
                                      kbd[:, k, g * HPG:(g + 1) * HPG, :].rearrange("p h m -> p (h m)"), start=True, stop=False)
                        for g in range(GROUPS):
                            last = pe.matmul(ps_s[:, g, 0:SW], ones_b[0:1, :], bias.to_broadcast([1, HPG, M]), start=False, stop=True)
                        last.then_inc(sc_done, 1)
                    if s.has(2):
                        need(pe, s, xt_copied, -1)
                        c = ctxT[:, s.slot(2), :]
                        pe.wait_ge(s_ctx[s.slot(2)], (s.turn(2) + 1) * 16)
                        pe.matmul(ps_t[:, 0:D], c[:, 0:P], wv_s[0:C, :], start=True, stop=True)
                        pe.matmul(ps_t[:, D:2 * D], c[:, P:2 * P], wv_s[0:C, :], start=True, stop=True)
                        pe.matmul(ps_t[:, 2 * D:2 * D + M], wk_s[0:C, :], c[:, KA:KA + M], start=True, stop=True)
                        pe.matmul(ps_t[:, 2 * D + M:2 * D + M + P], wq_s[:, :], xt[:, 1 - s.par(0), 0:P],
                                  start=True, stop=True).then_inc(vkq_done, 1)
                    if s.has(-1):
                        pr = prob[:, s.par(-1), :]
                        need(pe, s, exp_done)
                        need(pe, s, onorm_done)
                        for c in range(NC_A):
                            dst = (ps_ao, ps_bw)[c // 4]
                            if c == 4:
                                need(pe, s, wo_taken)
                            last = pe.transpose(dst[:, (c % 4) * P:(c % 4 + 1) * P], pr[:, c * P:(c + 1) * P], ident[:, :])
                            if c % 4 == 3:
                                last.then_inc((pa_done, pb_done)[c // 4], 1)
                    if s.has(-1) or s.has(-2):
                        need(pe, s, pc_copied, -1)
                        last = None
                        if s.has(-1):
                            for c in range(NC_B):
                                last = pe.transpose(ps_c[0:RB, c * P:(c + 1) * P], pr[:, HEADS * KA + c * RB:HEADS * KA + (c + 1) * RB], ident[:, :])
                        if s.has(-2):
                            need(pe, s, onorm_done)
                            last = pe.transpose(ps_c[:, 2 * P:3 * P],
                                                onorm[:, s.par(-2), :, :].rearrange("p h d -> p (h d)"), ident[:, :])
                        last.then_inc(pc_done, 1)
                    if s.has(3) or s.has(-4):
                        need(pe, s, vkq_copied)
                        need(pe, s, xt_copied, -1)
                        if s.has(3):
                            need(pe, s, xn1_done)
                            last = pe.transpose(ps_t[:, 0:P], xn1[:, s.par(3), :], ident[:, :])
                        if s.has(-4):
                            need(pe, s, xn2_done)
                            last = pe.transpose(ps_t[:, P:2 * P], xn2[:, s.par(-4), :], ident[:, :])
                        last.then_inc(xt_done, 1)
                    if s.has(-1):
                        need(pe, s, pa_copied)
                        need(pe, s, vbd_done, -2)
                        vb = vbd[:, s.slot(-1), :, :, :]
                        for c in range(NC_A):
                            if c == 4:
                                need(pe, s, pb_copied)
                            pe.matmul(ps_ao[:, 2 * c * VW:2 * (c + 1) * VW], probT[:, c * P:(c + 1) * P],
                                      vb[:, 0, 2 * c:2 * c + 2, :].rearrange("p h d -> p (h d)"),
                                      start=(c == 0), stop=False)
                        need(pe, s, pc_copied)
                        for c in range(NC_B):
                            last = pe.matmul(ps_ao[:, c * HPC * VW:(c + 1) * HPC * VW],
                                             probT[0:RB, 1024 + c * P:1024 + (c + 1) * P],
                                             vb[0:RB, 1, c * HPC:(c + 1) * HPC, :].rearrange("p h d -> p (h d)"),
                                             start=False, stop=(c == NC_B - 1))
                        last.then_inc(pv_done, 1)
                    if s.has(-2) or s.has(-6):
                        need(pe, s, pc_copied)
                        need(pe, s, pb_copied)
                        need(pe, s, xt_copied, -1)
                        need(pe, s, wo_taken)
                        if s.has(-2):
                            last = pe.matmul(ps_bw[:, 0:D], probT[:, 1280:1408], wo_s[:, :], start=True, stop=True)
                        if s.has(-5):
                            last = pe.matmul(ps_bw[:, D:D + E], xt[:, 1 - s.par(0), P:2 * P], wg_s[:, :], start=True, stop=True)
                        if s.has(-6):
                            need(pe, s, pick_done)
                            for col, lhs in ((D + E, ustri), (D + 2 * E, ones_b)):
                                for k in range(TOPK):
                                    last = pe.matmul(ps_bw[:, col:col + E], lhs[:, :], pick[:, s.par(-6), k, :],
                                                     start=(k == 0), stop=(k == TOPK - 1))
                        last.then_inc(wo_done, 1)
                run(pe, attend, step)

            @block.vector
            def _(dve):
                for t in (ps_ao, ps_bw, ps_c, ps_t):
                    last = dve.memset(t[:, :], 0.0)
                dve.wait_ge(s_mask, 16)
                dve.tensor_scalar(out=mask_b[:, :, :].rearrange("p b m -> p (b m)"), in0=mask_u8[:, :],
                                  scalar1=-1.0, scalar2=MASKED, op0=ALU.add, op1=ALU.mult).then_inc(const_dve, 1)
                dve.memset(mv[:, :, :, :], 1.0).then_inc(const_dve, 1)
                dve.wait_ge(const_pool, 10)
                dve.tensor_scalar(out=khead[:, :], in0=band[:, :], scalar1=SCALE, scalar2=None, op0=ALU.mult).then_inc(const_dve, 1)
                dve.wait_ge(const_dve, 3)
                dve.wait_ge(const_act, 1)
                dve.wait_ge(s_x[0], 16)

                def step(s):
                    if s.has(-2):
                        need(dve, s, pv_done, -1)
                        o = ps_ao[:, 0:HEADS * VW].rearrange("p (h d) -> p h d", d=VW)
                        dve.reciprocal(out=rden[:, s.par(0), :], in_=o[:, :, HD]).then_inc(rden_done, 1)
                        need(dve, s, rden_done)
                        dve.tensor_tensor(out=onorm[:, s.par(-2), :, :], in0=o[:, :, 0:HD],
                                          in1=rden[:, s.par(0), :].unsqueeze(2).to_broadcast([P, HEADS, HD]),
                                          op=ALU.mult).then_inc(onorm_done, 1)
                    if s.has(4):
                        if not s.looped and s.n(4) in XC[1:3]:
                            dve.wait_ge(s_x[XC.index(s.n(4))], 16)
                        dve.bn_stats(out=bnst[:, s.par(0), 0, :], in_=rows(x_all, s, 4)).then_inc(bn1_done, 1)
                    if s.has(-3):
                        need(dve, s, wo_done, -1)
                        dve.scalar_tensor_tensor(out=rows(x_all, s, -3), in0=ps_bw[:, 0:D], scalar=gains[:, 0:1],
                                                 in1=rows(x_all, s, -3), op0=ALU.mult, op1=ALU.add).then_inc(x1_done, 1)
                    if s.has(-8):
                        need(dve, s, prow_done, -1)
                        if s.looped or s.has(-10):
                            dve.wait_ge(scat[s.slot(-10)], (s.turn(-10) + 1) * (TOPK * 16))
                        with nc.allow_low_precision(reason="one term is not zero, a whole number below 2 ** 24"):
                            dve.tensor_reduce(out=dest[:, s.par(-8), :], in_=prow[:, s.par(-8), :, :], axis=AX_X,
                                              op=ALU.add).then_inc(dest_done, 1)
                    need(dve, s, wo_done, -1)
                    need(dve, s, next_done, -2)
                    need(dve, s, x1_done)
                    dve.tensor_copy(out=lrt[:, s.par(0), :, :].rearrange("p a e -> p (a e)"), in_=ps_bw[:, D:D + 3 * E]).then_inc(wo_taken, 1)
                    if s.has(-3):
                        dve.bn_stats(out=bnst[:, s.par(0), 1, :], in_=rows(x_all, s, -3)).then_inc(bn2_done, 1)
                    if s.has(3):
                        need(dve, s, rstd_done, -1)
                        need(dve, s, xt_done, -2)
                        need(dve, s, bn1_done)
                        need(dve, s, bn2_done)
                        k = s.slot(-1)
                        dve.tensor_scalar(out=xn1[:, s.par(3), :], in0=rows(x_all, s, 3), scalar1=mv[:, k, 0, 0:1],
                                          scalar2=rstd[:, k, 0:1], op0=ALU.subtract, op1=ALU.mult).then_inc(xn1_done, 1)
                    if s.has(-4):
                        need(dve, s, rstd_done, -1)
                        need(dve, s, wo_taken)
                        need(dve, s, m8_kept, -2)
                        need(dve, s, bn1_done)
                        need(dve, s, bn2_done)
                        k = s.slot(-1)
                        dve.tensor_scalar(out=xn2[:, s.par(-4), :], in0=rows(x_all, s, -4), scalar1=mv[:, k, 1, 0:1],
                                          scalar2=rstd[:, k, 1:2], op0=ALU.subtract, op1=ALU.mult).then_inc(xn2_done, 1)
                    if s.has(-6):
                        if not s.has(-4):
                            need(dve, s, wo_taken)
                            need(dve, s, m8_kept, -2)
                        dve.max(out=m8[:, s.par(-6), :], in_=lrt[:, s.par(0), 0, :]).then_inc(max8_done, 1)
                        need(dve, s, max8_done)
                        need(dve, s, pick_done, -2)
                        if s.looped or s.has(-10):
                            dve.wait_ge(scat[s.slot(-6)], (s.turn(-10) + 1) * (TOPK * 16))
                        k = s.slot(-3)
                        for c in range(TOPK):
                            last = dve.tensor_scalar(out=pay[:, s.slot(-6), c, 0:D], in0=rows(x_all, s, -6), scalar1=mv[:, k, 1, 0:1],
                                                     scalar2=rstd[:, k, 1:2], op0=ALU.subtract, op1=ALU.mult)
                        last.then_inc(pay_done, 1)
                        dve.max_index(out=ix8[:, s.par(-6), :], in_max=m8[:, s.par(-6), :], in_values=lrt[:, s.par(0), 0, :]).then_inc(ix8_done, 1)
                        need(dve, s, ix8_done)
                        need(dve, s, prow_done, -1)
                        dve.tensor_tensor(out=pick[:, s.par(-6), :, :], in0=iota_e[:, :, :],
                                          in1=ix8[:, s.par(-6), 0:TOPK].unsqueeze(2).to_broadcast([P, TOPK, E]),
                                          op=ALU.is_equal).then_inc(pick_done, 1)
                    if s.has(4) or s.has(-3):
                        if not s.has(3) or not s.has(-4):
                            need(dve, s, bn1_done)
                            need(dve, s, bn2_done)
                        if s.has(4):
                            last = dve.bn_aggr(out=mv[:, s.slot(0), 0, :], in_=bnst[:, s.par(0), 0, :])
                        if s.has(-3):
                            last = dve.bn_aggr(out=mv[:, s.slot(0), 1, :], in_=bnst[:, s.par(0), 1, :])
                        last.then_inc(mv_done, 1)
                    if s.has(0):
                        sc = ps_s[:, :, 0:SW].rearrange("p g (h m) -> p g h m", m=M)
                        need(dve, s, sc_done)
                        dve.tensor_reduce(out=smax[:, s.par(0), :].rearrange("p (g h) -> p g h", g=GROUPS), in_=sc, axis=AX_X,
                                          op=ALU.max).then_inc(max_done, 1)
                        need(dve, s, max_done)
                        need(dve, s, pc_done, -1)
                        for lo, hi in ((0, KA), (KA, M)):
                            part = prob[:, s.par(0), HEADS * lo:HEADS * hi].rearrange("p (g h m) -> p g h m", g=GROUPS, h=HPG)
                            top = smax[:, s.par(0), :].rearrange("p (g h) -> p g h", g=GROUPS).unsqueeze(3)
                            last = dve.tensor_tensor(out=part, in0=sc[:, :, :, lo:hi],
                                                     in1=top.to_broadcast([P, GROUPS, HPG, hi - lo]), op=ALU.subtract)
                        last.then_inc(sub_done, 1)
                    if s.has(2):
                        need(dve, s, sc_done)
                        need(dve, s, vkq_copied)
                        spread_keys(dve, s, 0, KBD_DVE).then_inc(kbd2_done, 1)

                def all_x():
                    for k in range(3, XN):
                        dve.wait_ge(s_x[k], 16)
                run(dve, attend, step, all_x)


        with ExitStack() as ps_es:
            def pb2(name, shape, dt=F32):
                return ps_es.enter_context(nc.psum_tensor(name, shape, dt))
            ps_x = pb2("ps_x", [P, 2, 512])
            ps_h = pb2("ps_h", [P, 4, 512])
            ps_y = pb2("ps_y", [P, 2, 512])
            block = ps_es.enter_context(nc.Block())

            def load_table(engine, values, which, lag, j, looped):
                n0 = j * experts.unroll
                first, last = lag, experts.unroll + lag
                if not looped:
                    first, last = max(first, -n0), min(last, TILES - n0)
                values.clear()
                if last > first:
                    cols = tile_i[0:1, which, bass.ds(n0 + first, last - first)] if looped else tile_i[0:1, which, n0 + first:n0 + last]
                    _, loaded = nc.values_load_multi_w_load_instructions(
                        cols, engines=[engine], min_val=0, max_val=(E - 1, E * SLOTS + (TILES_PAD - 1) * P)[which],
                        skip_runtime_bounds_check_because="the vector engine has clamped the experts, and the rows follow from "
                                                          "counts that add up to the tiles")
                    values.update(zip(range(first, last), loaded))

            TAB_TAIL, TAB_GATES, TAB_TILES = 1, 12, 13

            @block.sync
            def _(sp):
                sp.wait_ge(s_tab, TAB_TAIL)
                for e in range(E):
                    row = sp.value_load(eint[0:1, 0, e:e + 1], min_val=e * SLOTS, max_val=e * SLOTS + NTOK)
                    sp.dma_start(expert_in[bass.ds(row, P), :], padrow[:, :]).then_inc(s_tail, 16)
                sp.wait_ge(s_tail, (TILES_PAD + E) * 16)
                sp.wait_ge(s_tab, TAB_TILES)
                row_of = {}

                def step(s):
                    if s.has(3):
                        row = row_of[s.off + 3]
                        need(sp, s, to_done, -3)
                        sp.dma_start(xe[:, s.slot(3, 8), :], expert_in[bass.ds(row, P), :]).then_inc(xe_in[s.slot(3, 8)], 16)
                run(sp, experts, step, turn=lambda j, looped: load_table(mybir.EngineType.SP, row_of, 1, 3, j, looped))

            @block.gpsimd
            def _(pool):
                def step(s):
                    if s.has(-2) or s.has(-3):
                        need(pool, s, to_done, -1)
                    if s.has(-2):
                        need(pool, s, y_copied)
                        pool.tensor_tensor(out=to[:, s.slot(-2), :], in0=xe[:, s.slot(-2, 8), D:D + 1].bitcast(U32), in1=no_row[:, :],
                                           op=ALU.add).then_inc(to_done, 1)
                    if s.has(-3):
                        pool.indirect_dma_start(out=expert_out[:, :], out_offset=bass.IndirectOffsetOnAxis(ap=to[:, s.slot(-3), :], axis=0),
                                                in_=ye[:, s.slot(-3), :], in_offset=None, bounds_check=TOPK * NTOK - 1,
                                                oob_is_err=False).then_inc(y_out[s.slot(-3)], 16)
                run(pool, experts, step)
                for r in range(4):
                    pool.wait_ge(y_out[r], TILES // 4 * 16)

            @block.scalar
            def _(act):
                act.wait_ge(s_tab, TAB_GATES)
                act.activation(gate_d[:, :, :], gate_d[:, :, :], ACT.Exp).then_inc(s_gate, 1)

                def step(s):
                    if s.has(2):
                        need(act, s, xe_done)
                        act.activation(xeT[:, s.slot(2), :], ps_x[:, s.par(0), 0:P], ACT.Copy).then_inc(xe_copied, 1)
                    if s.has(0):
                        need(act, s, h_done)
                        need(act, s, f_done, -2)
                        act.activation(sg[:, s.par(0), :], ps_h[:, s.slot(0), 0:I], ACT.Silu).then_inc(silu_done, 1)
                run(act, experts, step)

            @block.tensor
            def _(pe):
                pe.wait_ge(s_tab, TAB_TILES)
                pe.wait_ge(s_wffn, (2 + E) * 16)

                expert_of = {}

                def step(s):
                    if s.has(2):
                        pe.wait_ge(xe_in[s.slot(2, 8)], (s.turn(2, 8) + 1) * 16)
                        need(pe, s, xe_copied, -2)
                        pe.transpose(ps_x[:, s.par(0), 0:P], xe[:, s.slot(2, 8), 0:D], ident[:, :]).then_inc(xe_done, 1)
                    if s.has(0):
                        need(pe, s, xe_copied, -2)
                        need(pe, s, w1_copied, -1)
                        need(pe, s, f_done, -4)
                        for c in range(2 * IC):
                            last = pe.matmul(ps_h[:, s.slot(0), c * P:(c + 1) * P], w1e[:, s.par(0), c * P:(c + 1) * P],
                                             xeT[:, s.slot(0), :], start=True, stop=True)
                        last.then_inc(h_done, 1)
                    if s.has(-2):
                        e = expert_of[s.off - 2]
                        need(pe, s, f_done, -2)
                        need(pe, s, y_copied, -2)
                        for c in range(IC):
                            last = pe.matmul(ps_y[:, s.par(0), 0:D], ff[:, s.slot(-2), c * P:(c + 1) * P],
                                             w2_s[:, bass.ds(e, 1), c, :].rearrange("p a n -> p (a n)"), start=(c == 0), stop=(c == IC - 1))
                        last.then_inc(y_done, 1)
                run(pe, experts, step, turn=lambda j, looped: load_table(mybir.EngineType.PE, expert_of, 0, -2, j, looped))

            @block.vector
            def _(dve):
                links = [0]

                def link(ins):
                    links[0] += 1
                    ins.then_inc(s_tab, 1)
                    dve.wait_ge(s_tab, links[0])

                dve.wait_ge(s_pad, 6)
                link(dve.tensor_copy(out=eint[:, 0, :], in_=nextrow[:, :]))
                link(dve.tensor_tensor(out=etab[:, 0, :], in0=nextrow[:, :], in1=eoff[:, :], op=ALU.subtract))
                link(dve.tensor_scalar(out=eint[:, 1, :], in0=etab[:, 0, :], scalar1=float(P - 1), scalar2=None, op0=ALU.add))
                link(dve.tensor_scalar(out=eint[:, 2, :], in0=eint[:, 1, :], scalar1=7, scalar2=None, op0=ALU.arith_shift_right))
                link(dve.tensor_copy(out=etab[:, 1, :], in_=eint[:, 2, :]))
                n_j = etab[:, 1, :].unsqueeze(1).to_broadcast([P, E, E])
                link(dve.tensor_tensor(out=past[:, 0:E, :], in0=n_j, in1=lower[:, :, :], op=ALU.mult))
                link(dve.tensor_reduce(out=etab[:, 2, :], in_=past[:, 0:E, :], axis=AX_X, op=ALU.add))
                link(dve.tensor_scalar(out=etab[:, 3, :], in0=etab[:, 1, :], scalar1=-float(P), scalar2=float(SLOTS), op0=ALU.mult, op1=ALU.add))
                link(dve.tensor_tensor(out=past[:, :, :], in0=iota_t[:, :].unsqueeze(2).to_broadcast([P, TILES, E]),
                                       in1=etab[:, 2, :].unsqueeze(1).to_broadcast([P, TILES, E]), op=ALU.is_ge))
                with nc.allow_low_precision(reason="whole numbers below 2 ** 24"):
                    dve.tensor_reduce(out=tile_f[:, 0, :], in_=past[:, :, :], axis=AX_X, op=ALU.add)
                    link(dve.tensor_tensor(out=pastr[:, :, :], in0=past[:, :, :],
                                           in1=etab[:, 3, :].unsqueeze(1).to_broadcast([P, TILES, E]), op=ALU.mult))
                    dve.tensor_scalar(out=tile_i[:, 0, :], in0=tile_f[:, 0, :], scalar1=float(E - 1), scalar2=None, op0=ALU.min)
                    link(dve.tensor_reduce(out=tile_f[:, 1, :], in_=pastr[:, :, :], axis=AX_X, op=ALU.add))
                    link(dve.tensor_tensor(out=gate_d[:, :, :], in0=m8_all[:, :, :],
                                           in1=m8_all[:, :, 0:1].to_broadcast([P, NB, E]), op=ALU.subtract))
                raise_tiles = dve.scalar_tensor_tensor(out=tile_i[:, 1, :], in0=iota_t[:, :], scalar=float(P), in1=tile_f[:, 1, :],
                                                       op0=ALU.mult, op1=ALU.add)
                link(raise_tiles)

                def gates():
                    dve.wait_ge(s_gate, 1)
                    link(dve.tensor_reduce(out=gate_s[:, 0, :], in_=gate_d[:, :, :], axis=AX_X, op=ALU.add))
                    link(dve.tensor_tensor(out=gate_s[:, 1, :], in0=gate_d[:, :, 0], in1=gate_d[:, :, 1], op=ALU.add))
                    link(dve.scalar_tensor_tensor(out=gate_s[:, 2, :], in0=gate_s[:, 0, :], scalar=GATE_EPS, in1=gate_s[:, 1, :],
                                                  op0=ALU.mult, op1=ALU.add))
                    link(dve.reciprocal(out=gate_s[:, 0, :], in_=gate_s[:, 2, :]))
                    for k in range(TOPK):
                        link(dve.scalar_tensor_tensor(out=gate_w[:, k, :], in0=gate_d[:, :, k], scalar=gains[:, 1:2], in1=gate_s[:, 0, :],
                                                      op0=ALU.mult, op1=ALU.mult))

                expert_of = {}

                def step(s):
                    if s.has(1):
                        e = expert_of[s.off + 1]
                        need(dve, s, h_done, -1)
                        dve.tensor_scalar(out=w1e[:, s.par(1), :], in0=w1_s[:, bass.ds(e, 1), :].rearrange("p a n -> p (a n)"),
                                          scalar1=1.0, scalar2=None, op0=ALU.mult).then_inc(w1_copied, 1)
                    if s.has(0):
                        need(dve, s, silu_done)
                        need(dve, s, y_done, -2)
                        dve.tensor_tensor(out=ff[:, s.slot(0), :], in0=sg[:, s.par(0), :], in1=ps_h[:, s.slot(0), I:2 * I],
                                          op=ALU.mult).then_inc(f_done, 1)
                    if s.has(-2):
                        if s.looped or s.has(-6):
                            dve.wait_ge(y_out[s.slot(-2)], (s.turn(-6) + 1) * 16)
                        need(dve, s, y_done)
                        dve.tensor_copy(out=ye[:, s.slot(-2), :], in_=ps_y[:, s.par(0), 0:D]).then_inc(y_copied, 1)
                gates()
                dve.wait_ge(s_wffn, (2 + E) * 16)
                run(dve, experts, step, turn=lambda j, looped: load_table(mybir.EngineType.DVE, expert_of, 0, 1, j, looped))

        NCH = NB // CB
        with nc.Block() as block:
            def chunk(t, j):
                return t[:, bass.ds(j * CB, CB), :]

            @block.sync
            def _(sp):
                def load(j, c):
                    for k in range(TOPK):
                        src = expert_out[bass.ds(j * (CB * T) + k * NTOK, CB * T), :].rearrange("(b t) d -> t b d", t=T)
                        sp.dma_start(yk[:, c, k, :, :], src).then_inc(s_y[c], 16)
                for c in range(YR):
                    load(c, c)
                with sp.Fori(0, NCH // YR - 1) as j:
                    for c in range(YR):
                        sp.wait_ge(s_sum, j * YR + (c + 1))
                        load(j * YR + (YR + c), c)

            @block.scalar
            def _(act):
                with act.Fori(0, NCH) as j:
                    act.wait_ge(s_sum, j + 1)
                    act.dma_start(out[bass.ds(j * CB, CB), :, :].rearrange("b t d -> t b d"), chunk(x_all, j)).then_inc(s_out, 16)
                act.wait_ge(s_out, NCH * 16)

            @block.vector
            def _(dve):
                with dve.Fori(0, NCH // YR) as j:
                    for c in range(YR):
                        dve.wait_ge(s_y[c], (j + 1) * (TOPK * 16))

                        def add(b, k, into, base):
                            i = j * (YR * CB) + (c * CB + b)
                            return dve.scalar_tensor_tensor(out=into, in0=yk[:, c, k, b, :], scalar=gate_w[:, k, bass.ds(i, 1)], in1=base,
                                                            op0=ALU.mult, op1=ALU.add)
                        for b in range(CB):
                            xb = chunk(x_all, j * YR + c)[:, b, :]
                            last = add(b, 0, yk[:, c, 0, b, :], xb)
                        last.then_inc(s_half_sum, 1)
                        dve.wait_ge(s_half_sum, j * YR + (c + 1))
                        for b in range(CB):
                            last = add(b, 1, chunk(x_all, j * YR + c)[:, b, :], yk[:, c, 0, b, :])
                        last.then_inc(s_sum, 1)


_INS = ['x', 'ctx_768', 'mask_BxS2_bf1', 'g_xattn', 'g_ffn', 'L0_xattn_Wq', 'L0_xattn_Wk', 'L0_xattn_Wv', 'L0_xattn_Wo',
        'L0_ffn_Wg', 'L0_ffn_W11', 'L0_ffn_W12', 'L0_ffn_W2']


def kernel(**inputs):
    import numpy as np
    import concourse.bacc as bacc
    from concourse.bass_utils import run_bass_kernel_spmd

    nc = bacc.Bacc("TRN2", target_bir_lowering=False, num_devices=1)
    arrays, args = {}, []
    for name in _INS:
        a = np.ascontiguousarray(inputs[name])
        if a.dtype == np.bool_:
            a = a.view(np.uint8)
        if name == "ctx_768":
            a = a.transpose(0, 2, 1)
            rest = [a[:, :, KA:]] * 8
            pad = np.zeros(a.shape[:2] + (2 * P - 2 * KA - sum(r.shape[2] for r in rest),), a.dtype)
            a = np.ascontiguousarray(np.concatenate([a[:, :, :KA], a[:, :, :KA], *rest, pad], axis=2))
        arrays[f"in_{name}"] = a
        args.append(nc.dram_tensor(f"in_{name}", a.shape, mybir.dt.from_np(a.dtype), kind="ExternalInput").ap())
    shape = arrays["in_x"].shape
    args.append(nc.dram_tensor("out", shape, F32, kind="ExternalOutput").ap())
    flamingo_block(nc, *args)
    r = run_bass_kernel_spmd(nc, [arrays], core_ids=[0])
    return r.results[0]["out"]
```

```python
from contextlib import ExitStack

import concourse.bass as bass
from concourse import mybir

P = 128
ALU = mybir.AluOpType
ACT = mybir.ActivationFunctionType
F32 = mybir.dt.float32
F32R = mybir.dt.float32r
BF16 = mybir.dt.bfloat16
U8 = mybir.dt.uint8
AX_X = mybir.AxisListType.X

HEADS = 16
TOPK = 2
U32 = mybir.dt.uint32
I32 = mybir.dt.int32
HD = 8
GROUPS = 4
HPG = HEADS // GROUPS
KA = 64
UNROLL = 4
LN_EPS = 1e-5
GATE_EPS = 1e-8
HIGH = 0xFFFFF000
MASKED = 3.3895313892515355e38


def flamingo_block(nc, x, ctx_in, mask, g_xattn, g_ffn, wq, wk, wv, wo, wg, w11, w12, w2, out):
    NB, T, D = x.shape
    C = ctx_in.shape[1]
    M = mask.shape[1]
    E, _, I = w11.shape
    KB = M - KA
    HPC = 8
    RB = HPC * KB
    NC_A = HEADS // 2
    NC_B = HEADS // HPC
    SW = HPG * M
    VW = HD + 1
    IC = I // P
    NTOK = NB * T
    TILES_PAD = E - 1
    TILES = TOPK * NTOK // P + TILES_PAD
    SCALE = float(HD) ** -0.5
    assert T == P and D == P and HEADS * HD == D and RB <= P and SW <= 512

    with ExitStack() as es:
        def sb(name, shape, dt=F32):
            return es.enter_context(nc.sbuf_tensor(name, shape, dt))

        def sem(name):
            return es.enter_context(nc.semaphore(name))

        x_all = sb("x_all", [P, NB, D])
        m8_all = sb("m8_all", [P, NB, E])
        wq_s = sb("wq_s", [P, D])
        wk_s = sb("wk_s", [P, D])
        wv_s = sb("wv_s", [P, D])
        wo_s = sb("wo_s", [P, D])
        wg_s = sb("wg_s", [P, E])
        w1_s = sb("w1_s", [P, E, 2 * I])
        w2_s = sb("w2_s", [P, E, IC, D])
        gains = sb("gains", [P, 2])
        ident = sb("ident", [P, P])
        SLOTS = NTOK + P
        ROW = D + 4
        expert_in = nc.dram_tensor("expert_in", [E * SLOTS + TILES_PAD * P, ROW], F32, kind="Internal")
        expert_out = nc.dram_tensor("expert_out", [TOPK * NTOK, D], F32, kind="Internal")
        pay = sb("pay", [P, UNROLL, TOPK, ROW])

        PADDING = 1 << 20
        padrow = sb("padrow", [P, ROW])
        eoff = sb("eoff", [P, E])
        etab = sb("etab", [P, 4, E])
        eint = sb("eint", [P, 3, E], I32)
        lower = sb("lower", [P, E, E])
        iota_t = sb("iota_t", [P, TILES])
        past = sb("past", [P, TILES, E])
        pastr = sb("pastr", [P, TILES, E])
        PACK_BITS = (E * SLOTS).bit_length()
        PACK = 1 << PACK_BITS
        tile_f = sb("tile_f", [P, TILES])
        tile_i = sb("tile_i", [P, 4, TILES], I32)
        TAB_TAIL, TAB_TILES = 1, 13
        gate_d = sb("gate_d", [P, NB, E])
        gate_s = sb("gate_s", [P, 3, NB])
        gate_w = sb("gate_w", [P, TOPK, NB])
        xe = sb("xe", [P, 8, ROW])
        xeT = sb("xeT", [P, 4, P])
        sg = sb("sg", [P, 2, I])
        w1e = sb("w1e", [P, 4, 2 * I])
        ff = sb("ff", [P, 4, I])
        ye = sb("ye", [P, 4, D])
        to = sb("to", [P, 4, 1], U32)
        no_row = sb("no_row", [P, 1], U32)
        YR = 8
        CB = 4
        yk = sb("yk", [P, YR, TOPK, CB, D])

        mask_u8 = sb("mask_u8", [P, NB * M], U8)
        mask_b = sb("mask_b", [P, NB, M], BF16)
        ones_b = sb("ones_b", [P, P], BF16)
        band = sb("band", [P, HEADS])
        khead = sb("khead", [P, HEADS])
        vhead = sb("vhead", [P, 2, HEADS])
        ctxT = sb("ctxT", [C, UNROLL, 2 * P])
        xn1 = sb("xn1", [P, 2, D])
        xn2 = sb("xn2", [P, 2, D])
        xt = sb("xt", [P, 2, 2 * P])
        vkq = sb("vkq", [P, 2, 2 * D + M + P])
        kq_high = sb("kq_high", [P, 2, M + P])
        kq_low = sb("kq_low", [P, 2, M + P], F32R)
        q_high = sb("q_high", [P, 2, P], F32R)
        kbd = sb("kbd", [P, 2, 2, HEADS, M], F32R)
        vbd = sb("vbd", [P, UNROLL, 2, HEADS, VW])
        prob = sb("prob", [P, 2, HEADS * M])
        smax = sb("smax", [P, 2, HEADS])
        probT = sb("probT", [P, 8 * P + 2 * P + P])
        rden = sb("rden", [P, 2, HEADS])
        onorm = sb("onorm", [P, 2, HEADS, HD])
        bnst = sb("bnst", [P, 2, 2, 6])
        mv = sb("mv", [P, UNROLL, 2, 2])
        vare = sb("vare", [P, UNROLL, 2])
        neg_mean = sb("neg_mean", [P, UNROLL, 2])
        neg_half = sb("neg_half", [P, 2])
        rstd = sb("rstd", [P, UNROLL, 2])
        shift = sb("shift", [P, UNROLL, 2])
        lrt = sb("lrt", [P, 2, 3, E])
        m8 = sb("m8", [P, 2, E])
        ix8 = sb("ix8", [P, 2, E], U32)
        pick = sb("pick", [P, 2, TOPK, E], BF16)
        iota_e = sb("iota_e", [P, TOPK, E])
        nextrow = sb("nextrow", [P, E])
        row8 = sb("row8", [P, 2, E])
        prow = sb("prow", [P, 2, TOPK, E])
        dest = sb("dest", [P, 2, TOPK], U32)
        ustri = sb("ustri", [P, P], BF16)
        turn_add = sb("turn_add", [P, TOPK], U32)

        s_x = [sem(f"s_x{i}") for i in range(6)]
        s_w = sem("s_w")
        s_wffn = sem("s_wffn")
        s_mask = sem("s_mask")
        s_ctx = [sem(f"s_ctx{i}") for i in range(UNROLL)]
        s_g = sem("s_g")
        const_early = sem("const_early")
        const_pool = sem("const_pool")
        mask_done = sem("mask_done")
        s_wo = sem("s_wo")
        wk_scaled = sem("wk_scaled")
        const_dve = sem("const_dve")
        const_act = sem("const_act")
        sc_done = sem("sc_done")
        sub_done = sem("sub_done")
        max_done = sem("max_done")
        exp_done = sem("exp_done")
        vkq_done = sem("vkq_done")
        vkq_copied = sem("vkq_copied")
        pa_done = sem("pa_done")
        pb_done = sem("pb_done")
        pc_done = sem("pc_done")
        pa_copied = sem("pa_copied")
        pb_copied = sem("pb_copied")
        pc_copied = sem("pc_copied")
        xt_done = sem("xt_done")
        xt_copied = sem("xt_copied")
        pv_done = sem("pv_done")
        wo_done = sem("wo_done")
        rden_done = sem("rden_done")
        onorm_done = sem("onorm_done")
        wo_taken = sem("wo_taken")
        x1_done = sem("x1_done")
        m8_kept = sem("m8_kept")
        max8_done = sem("max8_done")
        ix8_done = sem("ix8_done")
        pick_done = sem("pick_done")
        row8_done = sem("row8_done")
        prow_done = sem("prow_done")
        next_done = sem("next_done")
        dest_done = sem("dest_done")
        pay_done = sem("pay_done")
        tok_done = sem("tok_done")
        scat = [sem(f"scat{i}") for i in range(UNROLL)]
        s_pad = sem("s_pad")
        s_tail = sem("s_tail")
        s_tab = sem("s_tab")
        s_gate = sem("s_gate")
        s_gate_d = sem("s_gate_d")
        s_gate_exp = sem("s_gate_exp")
        xe_in = [sem(f"xe_in{i}") for i in range(8)]
        xe_done = sem("xe_done")
        xe_copied = sem("xe_copied")
        h_done = sem("h_done")
        silu_done = sem("silu_done")
        f_done = sem("f_done")
        w1_copied = sem("w1_copied")
        y_done = sem("y_done")
        y_copied = sem("y_copied")
        to_done = sem("to_done")
        y_out = [sem(f"y_out{i}") for i in range(4)]
        s_y = [sem(f"s_y{i}") for i in range(YR)]
        s_sum = sem("s_sum")
        s_out = sem("s_out")
        s_half_sum = sem("s_half_sum")
        s_scaled = sem("s_scaled")
        bn1_done = sem("bn1_done")
        bn2_done = sem("bn2_done")
        mv_done = sem("mv_done")
        var_done = sem("var_done")
        rstd_done = sem("rstd_done")
        shift_done = sem("shift_done")
        xn1_done = sem("xn1_done")
        xn2_done = sem("xn2_done")
        high_done = sem("high_done")
        low_done = sem("low_done")
        qh_done = sem("qh_done")
        kh_done = sem("kh_done")
        kl_done = sem("kl_done")
        vbd_done = sem("vbd_done")

        class Plan:
            def __init__(self, total, unroll, first, loop0, loop1, last):
                assert first % unroll == 0 and loop0 % unroll == 0 and loop1 % unroll == 0
                self.total, self.unroll, self.first, self.loop0, self.loop1, self.last = total, unroll, first, loop0, loop1, last

        class Step:
            def __init__(self, plan, j, off, looped):
                self.plan, self.j, self.off, self.looped = plan, j, off, looped

            def has(self, lag):
                return self.looped or 0 <= self.plan.unroll * self.j + self.off + lag < self.plan.total

            def at(self, n):
                return not self.looped and self.plan.unroll * self.j + self.off == n

            def n(self, k):
                return self.j * self.plan.unroll + (self.off + k)

            def par(self, lag):
                return (self.off + lag) % 2

            def slot(self, lag, ring=4):
                return (self.off + lag) % ring

            def turn(self, lag, ring=4):
                return self.j * (self.plan.unroll // ring) + (self.off + lag) // ring

        def run(eng, plan, step, before_loop=lambda: None, turn=lambda j, looped: None):
            u = plan.unroll
            for s in range(plan.first, plan.loop0):
                if s % u == 0:
                    turn(s // u, False)
                step(Step(plan, s // u, s % u, False))
            before_loop()
            with eng.Fori(plan.loop0 // u, plan.loop1 // u) as j:
                turn(j, True)
                for off in range(u):
                    step(Step(plan, j, off, True))
            for s in range(plan.loop1, plan.last + 1):
                if s % u == 0:
                    turn(s // u, False)
                step(Step(plan, s // u, s % u, False))

        FIRST, LOOP0 = -UNROLL, 3 * UNROLL
        attend = Plan(NB, UNROLL, FIRST, LOOP0, NB - 2 * UNROLL, NB + 7)
        experts = Plan(TILES, 16, -16, 16, (TILES - 4) // 16 * 16, TILES + 2)

        LAGS = {
            sc_done: (0,), max_done: (0,), sub_done: (0,), exp_done: (-1,), vkq_done: (2,), vkq_copied: (2,),
            pa_done: (-1,), pb_done: (-1,), pc_done: (-1, -2), pa_copied: (-1,), pb_copied: (-1,), pc_copied: (-1, -2),
            xt_done: (3, -4), xt_copied: (3, -4), pv_done: (-1,), wo_done: (-2, -6), rden_done: (-2,), onorm_done: (-2,),
            x1_done: (-3,), wo_taken: (4, -7), bn1_done: (4,), bn2_done: (-3,), mv_done: (4, -3), var_done: (4, -3), shift_done: (4, -3),
            rstd_done: (4, -3), xn1_done: (3,), xn2_done: (-4,), pay_done: (-5,), max8_done: (-6,), ix8_done: (-6,),
            m8_kept: (-6,), pick_done: (-6,), row8_done: (-7,), prow_done: (-7,), next_done: (-7,), dest_done: (-8,),
            tok_done: (-8,), high_done: (2,), qh_done: (1,), low_done: (2,), kh_done: (2,), kl_done: (1,), vbd_done: (1,),
            xe_done: (2,), xe_copied: (2,), h_done: (0,), silu_done: (0,), f_done: (0,), w1_copied: (2,),
            y_done: (-2,), y_copied: (-2,), to_done: (-2,),
        }

        def need(eng, s, signal, step=0):
            first, last = max(LAGS[signal]), min(LAGS[signal])
            if s.looped:
                eng.wait_ge(signal, s.n(step + first + 1))
                return
            count = min(s.n(step) + first + 1, s.plan.total + first - last)
            if count > 0:
                eng.wait_ge(signal, count)

        def batch(t, s, lag):
            return t[:, bass.ds(s.n(lag), 1)] if s.looped else t[:, s.n(lag):s.n(lag) + 1]

        def rows(t, s, lag):
            return batch(t, s, lag).rearrange("p a d -> p (a d)")

        XC = [0, 2, 6, LOOP0 + 4, 29, 46, NB]
        XN = len(XC) - 1
        MASKS_FIRST = 8
        EARLY, VALUES, ROUTING = 5, 4, 8

        def spread_keys(eng, s, lag, part):
            k = s.par(lag)
            return eng.tensor_tensor(out=kbd[:, k, part, :, :], in0=(kq_high, kq_low)[part][:, k, 0:M].unsqueeze(1).to_broadcast([P, HEADS, M]),
                                     in1=khead[:, :].unsqueeze(2).to_broadcast([P, HEADS, M]), op=ALU.mult)

        with ExitStack() as ps_es:
            def pb(name, shape, dt=F32):
                return ps_es.enter_context(nc.psum_tensor(name, shape, dt))
            ps_s = pb("ps_s", [P, GROUPS, 512])
            ps_ao = pb("ps_ao", [P, 512])
            ps_bw = pb("ps_bw", [P, 512])
            ps_c = pb("ps_c", [P, 512])
            ps_t = pb("ps_t", [P, 512])
            block = ps_es.enter_context(nc.Block())

            @block.sync
            def _(sp):
                def load_x(k):
                    sp.dma_start(x_all[:, XC[k]:XC[k + 1], :],
                                 x[XC[k]:XC[k + 1], :, :].rearrange("b t d -> t b d")).then_inc(s_x[k], 16)

                load_x(0)
                for dst, src in ((wv_s[0:C, :], wv), (wk_s[0:C, :], wk), (wq_s[:, :], wq)):
                    sp.dma_start(dst, src).then_inc(s_w, 16)
                load_x(1)
                for dst, src in ((wo_s[:, :], wo), (wg_s[:, :], wg)):
                    sp.dma_start(dst, src).then_inc(s_wo, 16)
                for k in range(2, XN):
                    load_x(k)
                sp.dma_start(w1_s[:, :, 0:I], w11.rearrange("e h i -> h e i")).then_inc(s_wffn, 16)
                sp.dma_start(w1_s[:, :, I:2 * I], w12.rearrange("e h i -> h e i")).then_inc(s_wffn, 16)
                for e in range(E):
                    sp.dma_start(w2_s[:, e, :, :], w2[e, :, :].rearrange("(c i) h -> i c h", c=IC)).then_inc(s_wffn, 16)
                sp.wait_ge(s_pad, 1)
                for k in range(TILES_PAD):
                    sp.dma_start(expert_in[E * SLOTS + k * P:E * SLOTS + (k + 1) * P, :], padrow[:, :]).then_inc(s_tail, 16)
                sp.wait_ge(s_tab, TAB_TAIL)
                _, ends = nc.values_load_multi_w_load_instructions(
                    eint[0:1, 0, :], engines=[mybir.EngineType.SP], min_val=0, max_val=E * SLOTS - P,
                    skip_runtime_bounds_check_because="an expert has at most NTOK rows of its NTOK + P")
                for row in ends:
                    sp.dma_start(expert_in[bass.ds(row, P), :], padrow[:, :]).then_inc(s_tail, 16)
                sp.wait_ge(s_tail, (TILES_PAD + E) * 16)

            @block.gpsimd
            def _(pool):
                pool.memset(ident[:, :], 0.0).then_inc(const_early, 1)
                pool.memset(band[:, :], 1.0).then_inc(const_early, 1)
                pool.memset(neg_half[:, :], -0.5)
                pool.wait_ge(const_early, 2)
                pool.affine_select(out=ident[:, :], in_=ident[:, :], compare_op=ALU.not_equal, fill=1.0,
                                   base=0, pattern=[[-1, P]], channel_multiplier=1).then_inc(const_early, 1)
                pool.affine_select(out=band[:, :], in_=band[:, :], compare_op=ALU.is_ge, fill=0.0,
                                   base=0, pattern=[[-HD, HEADS]], channel_multiplier=1).then_inc(const_early, 1)
                pool.wait_ge(const_early, 4)
                pool.affine_select(out=band[:, :], in_=band[:, :], compare_op=ALU.is_ge, fill=0.0,
                                   base=HD - 1, pattern=[[HD, HEADS]], channel_multiplier=-1).then_inc(const_early, 1)
                pool.wait_ge(const_early, EARLY)

                def constants_of_values():
                    pool.memset(vhead[:, :, :], 1.0).then_inc(const_pool, 1)
                    pool.memset(vbd[:, :, :, :, :], 1.0).then_inc(const_pool, 1)
                    pool.memset(ones_b[:, :], 1.0)
                    pool.wait_ge(const_pool, 2)
                    v = vhead[:, 0, :].rearrange("p (a b) -> p a b", b=2)
                    pool.affine_select(out=v[:, :, 0], in_=v[:, :, 0], compare_op=ALU.is_ge, fill=0.0,
                                       base=KA - 1, pattern=[[0, HEADS // 2]], channel_multiplier=-1)
                    pool.affine_select(out=v[:, :, 1], in_=v[:, :, 1], compare_op=ALU.is_ge, fill=0.0,
                                       base=-KA, pattern=[[0, HEADS // 2]], channel_multiplier=1)
                    w = vhead[:, 1, :].rearrange("p (a b) -> p a b", b=HPC)
                    pool.affine_select(out=w, in_=w, compare_op=ALU.is_ge, fill=0.0,
                                       base=0, pattern=[[0, NC_B], [-KB, HPC]], channel_multiplier=1).then_inc(const_pool, 1)
                    pool.wait_ge(const_pool, 3)
                    pool.affine_select(out=w, in_=w, compare_op=ALU.is_ge, fill=0.0,
                                       base=KB - 1, pattern=[[0, NC_B], [KB, HPC]], channel_multiplier=-1).then_inc(const_pool, 1)
                    pool.wait_ge(const_pool, VALUES)
                    for r in range(UNROLL):
                        pool.tensor_copy(out=vbd[:, r, :, :, HD], in_=vhead[:, :, :])

                def constants_of_routing():
                    pool.memset(ustri[:, :], 1.0).then_inc(const_pool, 1)
                    pool.memset(padrow[:, 0:D], 0.0)
                    pool.memset(padrow[:, D:ROW].bitcast(U32), PADDING).then_inc(s_pad, 1)
                    pool.memset(pay[:, :, :, :], 0.0).then_inc(const_pool, 1)
                    pool.memset(no_row[:, :], 0)
                    pool.memset(turn_add[:, :], UNROLL)
                    pool.memset(lower[:, :, :], 1.0).then_inc(const_pool, 1)
                    for rows_of in (nextrow, eoff):
                        pool.iota(rows_of[:, :], pattern=[[SLOTS, E]], base=0, channel_multiplier=0,
                                  allow_small_or_imprecise_dtypes=True)
                    pool.iota(iota_e[:, :, :], pattern=[[0, TOPK], [1, E]], base=0, channel_multiplier=0,
                              allow_small_or_imprecise_dtypes=True)
                    pool.iota(iota_t[:, :], pattern=[[1, TILES]], base=0, channel_multiplier=0,
                              allow_small_or_imprecise_dtypes=True)
                    pool.wait_ge(const_pool, VALUES + 3)
                    pool.affine_select(out=ustri[:, :], in_=ustri[:, :], compare_op=ALU.is_ge, fill=0.0,
                                       base=-1, pattern=[[1, P]], channel_multiplier=-1)
                    pool.affine_select(out=lower[:, :, :], in_=lower[:, :, :], compare_op=ALU.is_ge, fill=0.0,
                                       base=0, pattern=[[1, E], [-1, E]], channel_multiplier=0)
                    for r in range(UNROLL):
                        last = pool.iota(pay[:, r, :, D:D + 1].bitcast(I32), pattern=[[NTOK, TOPK]], base=r - UNROLL,
                                         channel_multiplier=NB, allow_small_or_imprecise_dtypes=True)
                    last.then_inc(const_pool, 1)
                    pool.wait_ge(const_pool, ROUTING)

                def step(s):
                    if s.at(-3):
                        constants_of_values()
                        pool.wait_ge(const_dve, 2)
                    if s.at(1):
                        constants_of_routing()
                    if s.has(1):
                        need(pool, s, sc_done, -1)
                        need(pool, s, low_done, -1)
                        spread_keys(pool, s, 1, 1).then_inc(kl_done, 1)
                    if s.has(1):
                        need(pool, s, vkq_copied, -1)
                        need(pool, s, pv_done, -2)
                        src = vkq[:, s.par(1), 0:2 * D].rearrange("p (c h d) -> p (c h) d", c=2, d=HD)
                        pool.tensor_tensor(out=vbd[:, s.slot(1), :, :, 0:HD].rearrange("p c h d -> p (c h) d"), in0=src,
                                           in1=vhead[:, :, :].rearrange("p c h -> p (c h)").unsqueeze(2).to_broadcast([P, 2 * HEADS, HD]),
                                           op=ALU.mult).then_inc(vbd_done, 1)
                    if s.has(4) or s.has(-3):
                        k = s.slot(0)
                        need(pool, s, var_done)
                        pool.tensor_tensor(out=rstd[:, k, :], in0=vare[:, k, :], in1=neg_half[:, :],
                                           op=ALU.pow).then_inc(rstd_done, 1)
                        need(pool, s, rstd_done)
                        pool.tensor_tensor(out=shift[:, k, :], in0=neg_mean[:, k, :], in1=rstd[:, k, :], op=ALU.mult).then_inc(shift_done, 1)
                    if s.has(-7):
                        k = s.par(-7)
                        need(pool, s, wo_taken)
                        need(pool, s, next_done, -1)
                        pool.tensor_tensor(out=row8[:, k, :], in0=lrt[:, s.par(0), 1, :], in1=nextrow[:, :], op=ALU.add).then_inc(row8_done, 1)
                        need(pool, s, row8_done)
                        pool.tensor_tensor(out=prow[:, k, :, :], in0=pick[:, k, :, :],
                                           in1=row8[:, k, :].unsqueeze(1).to_broadcast([P, TOPK, E]), op=ALU.mult).then_inc(prow_done, 1)
                        need(pool, s, prow_done)
                    if s.has(-8):
                        need(pool, s, pay_done, -3)
                        tok = pay[:, s.slot(-8), :, D:D + 1].bitcast(U32).rearrange("p k a -> p (k a)")
                        pool.tensor_tensor(out=tok, in0=tok, in1=turn_add[:, :], op=ALU.add).then_inc(tok_done, 1)
                        need(pool, s, dest_done)
                        need(pool, s, tok_done)
                    if s.has(-7):
                        pool.tensor_tensor(out=nextrow[:, :], in0=nextrow[:, :], in1=lrt[:, s.par(0), 2, :], op=ALU.add).then_inc(next_done, 1)
                    if s.has(-8):
                        for c in range(TOPK):
                            pool.indirect_dma_start(out=expert_in[:, :],
                                                    out_offset=bass.IndirectOffsetOnAxis(ap=dest[:, s.par(-8), c:c + 1], axis=0),
                                                    in_=pay[:, s.slot(-8), c, :], in_offset=None).then_inc(scat[s.slot(-8)], 16)

                run(pool, attend, step)
                for r in range(UNROLL):
                    pool.wait_ge(scat[r], NB // UNROLL * TOPK * 16)

            @block.scalar
            def _(act):
                def load_ctx(s, lag):
                    k = s.slot(lag)
                    src = ctx_in[bass.ds(s.n(lag), 1), :, :].rearrange("a c m -> (a c) m") if s.looped else ctx_in[s.n(lag), :, :]
                    act.dma_start(ctxT[:, k, :], src).then_inc(s_ctx[k], 16)

                for b in range(FIRST + 6):
                    load_ctx(Step(attend, 0, b, False), 0)
                act.dma_start(mask_u8[:, :], mask.rearrange("b m -> (b m)").unsqueeze(0).to_broadcast([P, NB * M])).then_inc(s_mask, 16)
                act.dma_start(gains[:, 0:1], g_xattn.unsqueeze(0).to_broadcast([P, 1])).then_inc(s_g, 16)
                act.dma_start(gains[:, 1:2], g_ffn.unsqueeze(0).to_broadcast([P, 1])).then_inc(s_g, 16)

                def step(s):
                    if s.at(-1):
                        act.wait_ge(s_g, 32)
                        act.activation(gains[:, :], gains[:, :], ACT.Tanh).then_inc(const_act, 1)
                    if s.has(-4):
                        need(act, s, shift_done, -1)
                        need(act, s, xt_done, -2)
                        need(act, s, pay_done, -1)
                        k = s.slot(-1)
                        act.activation(xn2[:, s.par(-4), :], rows(x_all, s, -4), ACT.Identity, bias=shift[:, k, 1:2],
                                       scale=rstd[:, k, 1:2]).then_inc(xn2_done, 1)
                    if s.has(3):
                        need(act, s, shift_done, -1)
                        need(act, s, xt_done, -2)
                        k = s.slot(-1)
                        act.activation(xn1[:, s.par(3), :], rows(x_all, s, 3), ACT.Identity, bias=shift[:, k, 0:1],
                                       scale=rstd[:, k, 0:1]).then_inc(xn1_done, 1)
                    if s.has(-1):
                        need(act, s, sub_done, -1)
                        act.activation(prob[:, s.par(-1), :], prob[:, s.par(-1), :], ACT.Exp).then_inc(exp_done, 1)
                    if s.has(2):
                        need(act, s, vkq_done)
                        need(act, s, vbd_done, -1)
                        need(act, s, low_done, -2)
                        act.activation(vkq[:, s.par(2), :], ps_t[:, 0:2 * D + M + P], ACT.Copy).then_inc(vkq_copied, 1)
                    if s.has(-1):
                        need(act, s, pa_done)
                        act.activation(probT[:, 0:512], ps_ao[:, :], ACT.Copy).then_inc(pa_copied, 1)
                        need(act, s, pb_done)
                        act.activation(probT[:, 512:1024], ps_bw[:, :], ACT.Copy).then_inc(pb_copied, 1)
                    if s.has(-1) or s.has(-2):
                        need(act, s, pc_done)
                        act.activation(probT[:, 1024:1408], ps_c[:, 0:384], ACT.Copy).then_inc(pc_copied, 1)
                    if s.has(3) or s.has(-4):
                        need(act, s, xt_done)
                        act.activation(xt[:, s.par(0), :], ps_t[:, 0:2 * P], ACT.Copy).then_inc(xt_copied, 1)
                    if s.has(1):
                        need(act, s, sc_done, -1)
                        need(act, s, high_done, -1)
                        act.activation(q_high[:, s.par(1), :], kq_high[:, s.par(1), M:], ACT.Copy).then_inc(qh_done, 1)
                    if s.has(-5):
                        if s.looped or s.has(-9):
                            act.wait_ge(scat[s.slot(-9)], (s.turn(-9) + 1) * (TOPK * 16))
                        need(act, s, xn2_done, -1)
                        if s.at(5):
                            act.wait_ge(const_pool, ROUTING)
                        act.activation(pay[:, s.slot(-5), :, 0:D], xn2[:, s.par(-5), :].unsqueeze(1).to_broadcast([P, TOPK, D]),
                                       ACT.Copy).then_inc(pay_done, 1)
                    if s.has(-6):
                        need(act, s, max8_done)
                        act.activation(rows(m8_all, s, -6), m8[:, s.par(-6), :], ACT.Copy).then_inc(m8_kept, 1)
                    if s.has(6):
                        need(act, s, vkq_done)
                        load_ctx(s, 6)
                run(act, attend, step)
                act.wait_ge(s_gate_d, 1)
                act.activation(gate_d[:, :, :], gate_d[:, :, :], ACT.Exp).then_inc(s_gate_exp, 1)
                act.activation(sg[:, 0, 0:2], gains[:, :], ACT.Silu)

            @block.tensor
            def _(pe):
                pe.wait_ge(const_early, 4)
                pe.wait_ge(const_dve, 1)

                def step(s):
                    if s.at(-2):
                        pe.wait_ge(s_w, 3 * 16)
                        pe.wait_ge(wk_scaled, 1)
                    if s.at(0):
                        pe.wait_ge(mask_done, 1)
                        pe.wait_ge(s_wo, 2 * 16)
                    if s.at(6):
                        pe.wait_ge(const_pool, ROUTING)
                    if s.at(MASKS_FIRST):
                        pe.wait_ge(mask_done, 2)
                    if s.has(0):
                        k = s.par(0)
                        need(pe, s, low_done, -2)
                        need(pe, s, kh_done, -2)
                        need(pe, s, kl_done, -1)
                        need(pe, s, qh_done, -1)
                        need(pe, s, sub_done, -1)
                        bias = mask_b[0:1, bass.ds(s.n(0), 1), :] if s.looped else mask_b[0:1, s.n(0):s.n(1), :]
                        for q_part, k_part in ((0, 0), (0, 1), (1, 0)):
                            for g in range(GROUPS):
                                pe.matmul(ps_s[:, g, 0:SW], (q_high[:, k, :], kq_low[:, k, M:])[q_part],
                                          kbd[:, k, k_part, g * HPG:(g + 1) * HPG, :].rearrange("p h m -> p (h m)"),
                                          start=(q_part == 0 and k_part == 0), stop=False)
                        for g in range(GROUPS):
                            last = pe.matmul(ps_s[:, g, 0:SW], ones_b[0:1, :], bias.to_broadcast([1, HPG, M]), start=False, stop=True)
                        last.then_inc(sc_done, 1)
                    if s.has(2):
                        need(pe, s, xt_copied, -1)
                        c = ctxT[:, s.slot(2), :]
                        pe.wait_ge(s_ctx[s.slot(2)], (s.turn(2) + 1) * 16)
                        pe.matmul(ps_t[:, 0:D], c[:, 0:P], wv_s[0:C, :], start=True, stop=True)
                        pe.matmul(ps_t[:, D:2 * D], c[:, P:2 * P], wv_s[0:C, :], start=True, stop=True)
                        pe.matmul(ps_t[:, 2 * D:2 * D + M], wk_s[0:C, :], c[:, KA:KA + M], start=True, stop=True)
                        pe.matmul(ps_t[:, 2 * D + M:2 * D + M + P], wq_s[:, :], xt[:, 1 - s.par(0), 0:P],
                                  start=True, stop=True).then_inc(vkq_done, 1)
                    if s.has(-1):
                        pr = prob[:, s.par(-1), :]
                        need(pe, s, exp_done)
                        need(pe, s, onorm_done)
                        for c in range(NC_A):
                            dst = (ps_ao, ps_bw)[c // 4]
                            if c == 4:
                                need(pe, s, wo_taken)
                            last = pe.transpose(dst[:, (c % 4) * P:(c % 4 + 1) * P], pr[:, c * P:(c + 1) * P], ident[:, :])
                            if c % 4 == 3:
                                last.then_inc((pa_done, pb_done)[c // 4], 1)
                    if s.has(-1) or s.has(-2):
                        need(pe, s, pc_copied, -1)
                        last = None
                        if s.has(-1):
                            for c in range(NC_B):
                                last = pe.transpose(ps_c[0:RB, c * P:(c + 1) * P], pr[:, HEADS * KA + c * RB:HEADS * KA + (c + 1) * RB], ident[:, :])
                        if s.has(-2):
                            need(pe, s, onorm_done)
                            last = pe.transpose(ps_c[:, 2 * P:3 * P],
                                                onorm[:, s.par(-2), :, :].rearrange("p h d -> p (h d)"), ident[:, :])
                        last.then_inc(pc_done, 1)
                    if s.has(3) or s.has(-4):
                        need(pe, s, vkq_copied)
                        need(pe, s, xt_copied, -1)
                        if s.has(3):
                            need(pe, s, xn1_done)
                            last = pe.transpose(ps_t[:, 0:P], xn1[:, s.par(3), :], ident[:, :])
                        if s.has(-4):
                            need(pe, s, xn2_done)
                            last = pe.transpose(ps_t[:, P:2 * P], xn2[:, s.par(-4), :], ident[:, :])
                        last.then_inc(xt_done, 1)
                    if s.has(-1):
                        need(pe, s, pa_copied)
                        need(pe, s, vbd_done, -2)
                        vb = vbd[:, s.slot(-1), :, :, :]
                        for c in range(NC_A):
                            if c == 4:
                                need(pe, s, pb_copied)
                            pe.matmul(ps_ao[:, 2 * c * VW:2 * (c + 1) * VW], probT[:, c * P:(c + 1) * P],
                                      vb[:, 0, 2 * c:2 * c + 2, :].rearrange("p h d -> p (h d)"),
                                      start=(c == 0), stop=False)
                        need(pe, s, pc_copied)
                        for c in range(NC_B):
                            last = pe.matmul(ps_ao[:, c * HPC * VW:(c + 1) * HPC * VW],
                                             probT[0:RB, 1024 + c * P:1024 + (c + 1) * P],
                                             vb[0:RB, 1, c * HPC:(c + 1) * HPC, :].rearrange("p h d -> p (h d)"),
                                             start=False, stop=(c == NC_B - 1))
                        last.then_inc(pv_done, 1)
                    if s.has(-2) or s.has(-6):
                        need(pe, s, pc_copied)
                        need(pe, s, pb_copied)
                        need(pe, s, xt_copied, -1)
                        need(pe, s, wo_taken)
                        if s.has(-2):
                            last = pe.matmul(ps_bw[:, 0:D], probT[:, 1280:1408], wo_s[:, :], start=True, stop=True)
                        if s.has(-5):
                            last = pe.matmul(ps_bw[:, D:D + E], xt[:, 1 - s.par(0), P:2 * P], wg_s[:, :], start=True, stop=True)
                        if s.has(-6):
                            need(pe, s, pick_done)
                            for col, lhs in ((D + E, ustri), (D + 2 * E, ones_b)):
                                for k in range(TOPK):
                                    last = pe.matmul(ps_bw[:, col:col + E], lhs[:, :], pick[:, s.par(-6), k, :],
                                                     start=(k == 0), stop=(k == TOPK - 1))
                        last.then_inc(wo_done, 1)
                run(pe, attend, step)

            @block.vector
            def _(dve):
                dve.memset(ps_t[:, 0:2 * P], 0.0)
                dve.memset(ps_bw[:, D:D + 3 * E], 0.0)
                dve.memset(ps_c[:, 0:3 * P], 0.0)
                dve.memset(mv[:, :, :, :], 1.0).then_inc(const_dve, 1)
                dve.wait_ge(const_early, EARLY)
                dve.tensor_copy(out=khead[:, :], in_=band[:, :]).then_inc(const_dve, 1)
                dve.wait_ge(const_dve, 2)
                dve.wait_ge(s_x[0], 16)

                def make_mask(lo, hi):
                    dve.tensor_scalar(out=mask_b[:, lo:hi, :].rearrange("p b m -> p (b m)"), in0=mask_u8[:, lo * M:hi * M],
                                      scalar1=-1.0, scalar2=MASKED, op0=ALU.add, op1=ALU.mult).then_inc(mask_done, 1)

                def step(s):
                    if s.at(NB + 7):
                        dve.wait_ge(m8_kept, NB)
                        dve.tensor_tensor(out=gate_d[:, :, :], in0=m8_all[:, :, :],
                                          in1=m8_all[:, :, 0:1].to_broadcast([P, NB, E]), op=ALU.subtract).then_inc(s_gate_d, 1)
                    if s.at(-3):
                        dve.wait_ge(s_w, 3 * 16)
                        dve.tensor_scalar(out=wk_s[0:C, :], in0=wk_s[0:C, :], scalar1=SCALE, scalar2=None,
                                          op0=ALU.mult).then_inc(wk_scaled, 1)
                    if s.at(-2):
                        dve.wait_ge(s_mask, 16)
                        make_mask(0, MASKS_FIRST)
                    if s.at(4):
                        make_mask(MASKS_FIRST, NB)
                    if s.at(3):
                        dve.wait_ge(const_act, 1)
                    if s.at(6):
                        dve.wait_ge(const_pool, ROUTING)
                    if s.has(-3):
                        need(dve, s, wo_done, -1)
                        dve.scalar_tensor_tensor(out=rows(x_all, s, -3), in0=ps_bw[:, 0:D], scalar=gains[:, 0:1],
                                                 in1=rows(x_all, s, -3), op0=ALU.mult, op1=ALU.add).then_inc(x1_done, 1)
                    if s.at(2):
                        need(dve, s, pv_done, -1)
                    need(dve, s, wo_done, -1)
                    need(dve, s, next_done, -2)
                    dve.tensor_copy(out=lrt[:, s.par(0), :, :].rearrange("p a e -> p (a e)"), in_=ps_bw[:, D:D + 3 * E]).then_inc(wo_taken, 1)
                    need(dve, s, m8_kept, -2)
                    need(dve, s, wo_taken)
                    if s.has(-8):
                        need(dve, s, prow_done, -1)
                        if s.looped or s.has(-10):
                            dve.wait_ge(scat[s.slot(-10)], (s.turn(-10) + 1) * (TOPK * 16))
                        with nc.allow_low_precision(reason="one term is not zero, a whole number below 2 ** 24"):
                            dve.tensor_reduce(out=dest[:, s.par(-8), :], in_=prow[:, s.par(-8), :, :], axis=AX_X,
                                              op=ALU.add).then_inc(dest_done, 1)
                    if s.has(-3):
                        dve.bn_stats(out=bnst[:, s.par(0), 1, :], in_=rows(x_all, s, -3)).then_inc(bn2_done, 1)
                    if s.has(-6):
                        dve.max(out=m8[:, s.par(-6), :], in_=lrt[:, s.par(0), 0, :]).then_inc(max8_done, 1)
                    if s.has(4):
                        if not s.looped and s.n(4) in XC[1:3]:
                            dve.wait_ge(s_x[XC.index(s.n(4))], 16)
                        dve.bn_stats(out=bnst[:, s.par(0), 0, :], in_=rows(x_all, s, 4)).then_inc(bn1_done, 1)
                    if s.has(-2):
                        need(dve, s, pv_done, -1)
                        o = ps_ao[:, 0:HEADS * VW].rearrange("p (h d) -> p h d", d=VW)
                        dve.reciprocal(out=rden[:, s.par(0), :], in_=o[:, :, HD]).then_inc(rden_done, 1)
                    if s.has(-6):
                        need(dve, s, pick_done, -2)
                    if not s.has(-2):
                        if s.has(4):
                            need(dve, s, bn1_done)
                        if s.has(-3):
                            need(dve, s, bn2_done)
                        if s.has(-6):
                            need(dve, s, max8_done)
                    if s.has(-2):
                        need(dve, s, rden_done)
                        dve.tensor_tensor(out=onorm[:, s.par(-2), :, :], in0=o[:, :, 0:HD],
                                          in1=rden[:, s.par(0), :].unsqueeze(2).to_broadcast([P, HEADS, HD]),
                                          op=ALU.mult).then_inc(onorm_done, 1)
                    if s.has(4):
                        last = dve.bn_aggr(out=mv[:, s.slot(0), 0, :], in_=bnst[:, s.par(0), 0, :])
                    if s.has(-3):
                        last = dve.bn_aggr(out=mv[:, s.slot(0), 1, :], in_=bnst[:, s.par(0), 1, :])
                    if s.has(4) or s.has(-3):
                        last.then_inc(mv_done, 1)
                    if s.has(-6):
                        dve.max_index(out=ix8[:, s.par(-6), :], in_max=m8[:, s.par(-6), :], in_values=lrt[:, s.par(0), 0, :]).then_inc(ix8_done, 1)
                    if s.has(4) or s.has(-3):
                        need(dve, s, mv_done)
                        k = s.slot(0)
                        dve.tensor_scalar(out=neg_mean[:, k, :], in0=mv[:, k, :, 0], scalar1=-1.0, scalar2=None, op0=ALU.mult)
                        dve.tensor_scalar(out=vare[:, k, :], in0=mv[:, k, :, 1], scalar1=LN_EPS, scalar2=None,
                                          op0=ALU.add).then_inc(var_done, 1)
                    if s.has(-6):
                        if not s.has(-8):
                            need(dve, s, prow_done, -1)
                        need(dve, s, ix8_done)
                        dve.tensor_tensor(out=pick[:, s.par(-6), :, :], in0=iota_e[:, :, :],
                                          in1=ix8[:, s.par(-6), 0:TOPK].unsqueeze(2).to_broadcast([P, TOPK, E]),
                                          op=ALU.is_equal).then_inc(pick_done, 1)
                    if s.has(0):
                        sc = ps_s[:, :, 0:SW].rearrange("p g (h m) -> p g h m", m=M)
                        need(dve, s, sc_done)
                        dve.tensor_reduce(out=smax[:, s.par(0), :].rearrange("p (g h) -> p g h", g=GROUPS), in_=sc, axis=AX_X,
                                          op=ALU.max).then_inc(max_done, 1)
                        need(dve, s, max_done)
                        need(dve, s, pc_done, -1)
                        for lo, hi in ((0, KA), (KA, M)):
                            part = prob[:, s.par(0), HEADS * lo:HEADS * hi].rearrange("p (g h m) -> p g h m", g=GROUPS, h=HPG)
                            top = smax[:, s.par(0), :].rearrange("p (g h) -> p g h", g=GROUPS).unsqueeze(3)
                            last = dve.tensor_tensor(out=part, in0=sc[:, :, :, lo:hi],
                                                     in1=top.to_broadcast([P, GROUPS, HPG, hi - lo]), op=ALU.subtract)
                        last.then_inc(sub_done, 1)
                    if s.has(2):
                        need(dve, s, sc_done)
                        need(dve, s, kl_done, -1)
                        need(dve, s, qh_done, -1)
                        need(dve, s, vkq_copied)
                        k = s.par(2)
                        both = vkq[:, k, 2 * D:2 * D + M + P]
                        dve.tensor_scalar(out=kq_high[:, k, :].bitcast(U32), in0=both.bitcast(U32), scalar1=HIGH, scalar2=None,
                                          op0=ALU.bitwise_and).then_inc(high_done, 1)
                        need(dve, s, high_done)
                        dve.tensor_tensor(out=kq_low[:, k, :], in0=both, in1=kq_high[:, k, :], op=ALU.subtract).then_inc(low_done, 1)
                        spread_keys(dve, s, 2, 0).then_inc(kh_done, 1)

                def all_x():
                    for k in range(3, XN):
                        dve.wait_ge(s_x[k], 16)
                run(dve, attend, step, all_x)

                links = [0]

                def link(ins):
                    links[0] += 1
                    ins.then_inc(s_tab, 1)
                    dve.wait_ge(s_tab, links[0])

                dve.wait_ge(next_done, NB)
                link(dve.tensor_copy(out=eint[:, 0, :], in_=nextrow[:, :]))
                link(dve.tensor_tensor(out=etab[:, 0, :], in0=nextrow[:, :], in1=eoff[:, :], op=ALU.subtract))
                link(dve.tensor_scalar(out=eint[:, 1, :], in0=etab[:, 0, :], scalar1=float(P - 1), scalar2=None, op0=ALU.add))
                link(dve.tensor_scalar(out=eint[:, 2, :], in0=eint[:, 1, :], scalar1=7, scalar2=None, op0=ALU.arith_shift_right))
                link(dve.tensor_copy(out=etab[:, 1, :], in_=eint[:, 2, :]))
                n_j = etab[:, 1, :].unsqueeze(1).to_broadcast([P, E, E])
                link(dve.tensor_tensor(out=past[:, 0:E, :], in0=n_j, in1=lower[:, :, :], op=ALU.mult))
                dve.tensor_reduce(out=etab[:, 2, :], in_=past[:, 0:E, :], axis=AX_X, op=ALU.add)
                link(dve.tensor_scalar(out=etab[:, 3, :], in0=etab[:, 1, :], scalar1=-float(P), scalar2=float(PACK + SLOTS),
                                       op0=ALU.mult, op1=ALU.add))
                link(dve.tensor_tensor(out=past[:, :, :], in0=iota_t[:, :].unsqueeze(2).to_broadcast([P, TILES, E]),
                                       in1=etab[:, 2, :].unsqueeze(1).to_broadcast([P, TILES, E]), op=ALU.is_ge))
                link(dve.tensor_tensor(out=pastr[:, :, :], in0=past[:, :, :],
                                       in1=etab[:, 3, :].unsqueeze(1).to_broadcast([P, TILES, E]), op=ALU.mult))
                with nc.allow_low_precision(reason="whole numbers below 2 ** 24"):
                    link(dve.tensor_reduce(out=tile_i[:, 2, :], in_=pastr[:, :, :], axis=AX_X, op=ALU.add))
                link(dve.tensor_scalar(out=tile_i[:, 3, :], in0=tile_i[:, 2, :], scalar1=PACK_BITS, scalar2=None, op0=ALU.arith_shift_right))
                dve.tensor_scalar(out=tile_i[:, 0, :], in0=tile_i[:, 3, :], scalar1=float(E - 1), scalar2=None, op0=ALU.min)
                link(dve.scalar_tensor_tensor(out=tile_f[:, :], in0=tile_i[:, 3, :], scalar=-float(PACK), in1=tile_i[:, 2, :],
                                              op0=ALU.mult, op1=ALU.add))
                link(dve.scalar_tensor_tensor(out=tile_i[:, 1, :], in0=iota_t[:, :], scalar=float(P), in1=tile_f[:, :],
                                              op0=ALU.mult, op1=ALU.add))
                assert links[0] == TAB_TILES


        with ExitStack() as ps_es:
            def pb2(name, shape, dt=F32):
                return ps_es.enter_context(nc.psum_tensor(name, shape, dt))
            ps_x = pb2("ps_x", [P, 2, 512])
            ps_h = pb2("ps_h", [P, 4, 512])
            ps_y = pb2("ps_y", [P, 2, 512])
            block = ps_es.enter_context(nc.Block())

            def load_table(engine, values, which, lag, j, looped):
                n0 = j * experts.unroll
                first, last = lag, experts.unroll + lag
                if not looped:
                    first, last = max(first, -n0), min(last, TILES - n0)
                values.clear()
                if last > first:
                    cols = tile_i[0:1, which, bass.ds(n0 + first, last - first)] if looped else tile_i[0:1, which, n0 + first:n0 + last]
                    _, loaded = nc.values_load_multi_w_load_instructions(
                        cols, engines=[engine], min_val=0, max_val=(E - 1, E * SLOTS + (TILES_PAD - 1) * P)[which],
                        skip_runtime_bounds_check_because="the vector engine has clamped the experts, and the rows follow from "
                                                          "counts that add up to the tiles")
                    values.update(zip(range(first, last), loaded))


            @block.sync
            def _(sp):
                row_of = {}

                def step(s):
                    if s.has(3):
                        row = row_of[s.off + 3]
                        need(sp, s, to_done, -3)
                        sp.dma_start(xe[:, s.slot(3, 8), :], expert_in[bass.ds(row, P), :]).then_inc(xe_in[s.slot(3, 8)], 16)
                run(sp, experts, step, turn=lambda j, looped: load_table(mybir.EngineType.SP, row_of, 1, 3, j, looped))

            @block.gpsimd
            def _(pool):
                def step(s):
                    if s.has(-2) or s.has(-3):
                        need(pool, s, to_done, -1)
                    if s.has(-2):
                        need(pool, s, y_copied)
                        pool.tensor_tensor(out=to[:, s.slot(-2), :], in0=xe[:, s.slot(-2, 8), D:D + 1].bitcast(U32), in1=no_row[:, :],
                                           op=ALU.add).then_inc(to_done, 1)
                    if s.has(-3):
                        pool.indirect_dma_start(out=expert_out[:, :], out_offset=bass.IndirectOffsetOnAxis(ap=to[:, s.slot(-3), :], axis=0),
                                                in_=ye[:, s.slot(-3), :], in_offset=None, bounds_check=TOPK * NTOK - 1,
                                                oob_is_err=False).then_inc(y_out[s.slot(-3)], 16)
                run(pool, experts, step)
                for r in range(4):
                    pool.wait_ge(y_out[r], (TILES - r + 3) // 4 * 16)

            @block.scalar
            def _(act):
                def step(s):
                    if s.has(2):
                        need(act, s, xe_done)
                        act.activation(xeT[:, s.slot(2), :], ps_x[:, s.par(0), 0:P], ACT.Copy).then_inc(xe_copied, 1)
                    if s.has(0):
                        need(act, s, h_done)
                        need(act, s, f_done, -2)
                        act.activation(sg[:, s.par(0), :], ps_h[:, s.slot(0), 0:I], ACT.Silu).then_inc(silu_done, 1)
                run(act, experts, step)

            @block.tensor
            def _(pe):
                pe.wait_ge(s_wffn, (2 + E) * 16)

                expert_of = {}

                def step(s):
                    if s.has(2):
                        pe.wait_ge(xe_in[s.slot(2, 8)], (s.turn(2, 8) + 1) * 16)
                        need(pe, s, xe_copied, -2)
                        pe.transpose(ps_x[:, s.par(0), 0:P], xe[:, s.slot(2, 8), 0:D], ident[:, :]).then_inc(xe_done, 1)
                    if s.has(0):
                        need(pe, s, xe_copied, -2)
                        need(pe, s, w1_copied, -2)
                        need(pe, s, f_done, -4)
                        for c in range(2 * IC):
                            last = pe.matmul(ps_h[:, s.slot(0), c * P:(c + 1) * P], w1e[:, s.slot(0), c * P:(c + 1) * P],
                                             xeT[:, s.slot(0), :], start=True, stop=True)
                        last.then_inc(h_done, 1)
                    if s.off == 0:
                        load_table(mybir.EngineType.PE, expert_of, 0, -2, s.j, s.looped)
                    if s.has(-2):
                        e = expert_of[s.off - 2]
                        need(pe, s, f_done, -2)
                        need(pe, s, y_copied, -2)
                        for c in range(IC):
                            last = pe.matmul(ps_y[:, s.par(0), 0:D], ff[:, s.slot(-2), c * P:(c + 1) * P],
                                             w2_s[:, bass.ds(e, 1), c, :].rearrange("p a n -> p (a n)"), start=(c == 0), stop=(c == IC - 1))
                        last.then_inc(y_done, 1)
                run(pe, experts, step)

            @block.vector
            def _(dve):
                gate_links = [0]

                def link(ins):
                    gate_links[0] += 1
                    ins.then_inc(s_gate, 1)
                    dve.wait_ge(s_gate, gate_links[0])

                def gates():
                    dve.wait_ge(s_gate_exp, 1)
                    link(dve.tensor_reduce(out=gate_s[:, 0, :], in_=gate_d[:, :, :], axis=AX_X, op=ALU.add))
                    link(dve.tensor_tensor(out=gate_s[:, 1, :], in0=gate_d[:, :, 0], in1=gate_d[:, :, 1], op=ALU.add))
                    link(dve.scalar_tensor_tensor(out=gate_s[:, 2, :], in0=gate_s[:, 0, :], scalar=GATE_EPS, in1=gate_s[:, 1, :],
                                                  op0=ALU.mult, op1=ALU.add))
                    link(dve.reciprocal(out=gate_s[:, 0, :], in_=gate_s[:, 2, :]))
                    for k in range(TOPK):
                        link(dve.scalar_tensor_tensor(out=gate_w[:, k, :], in0=gate_d[:, :, k], scalar=gains[:, 1:2], in1=gate_s[:, 0, :],
                                                      op0=ALU.mult, op1=ALU.mult))

                expert_of = {}

                def step(s):
                    if s.has(0):
                        need(dve, s, silu_done)
                        need(dve, s, y_done, -2)
                        dve.tensor_tensor(out=ff[:, s.slot(0), :], in0=sg[:, s.par(0), :], in1=ps_h[:, s.slot(0), I:2 * I],
                                          op=ALU.mult).then_inc(f_done, 1)
                    if s.has(-2):
                        if s.looped or s.has(-6):
                            dve.wait_ge(y_out[s.slot(-2)], (s.turn(-6) + 1) * 16)
                        need(dve, s, y_done)
                        dve.tensor_copy(out=ye[:, s.slot(-2), :], in_=ps_y[:, s.par(0), 0:D]).then_inc(y_copied, 1)
                    if s.off == 0:
                        load_table(mybir.EngineType.DVE, expert_of, 0, 2, s.j, s.looped)
                    if s.has(2):
                        e = expert_of[s.off + 2]
                        need(dve, s, h_done, -2)
                        dve.tensor_scalar(out=w1e[:, s.slot(2), :], in0=w1_s[:, bass.ds(e, 1), :].rearrange("p a n -> p (a n)"),
                                          scalar1=1.0, scalar2=None, op0=ALU.mult).then_inc(w1_copied, 1)
                gates()
                dve.wait_ge(s_wffn, (2 + E) * 16)
                run(dve, experts, step)

        NCH = NB // CB
        with nc.Block() as block:
            def chunk(t, j):
                return t[:, bass.ds(j * CB, CB), :]

            @block.sync
            def _(sp):
                def load(j, c):
                    for k in range(TOPK):
                        src = expert_out[k * NTOK:(k + 1) * NTOK, :].rearrange("(t b) d -> t b d", b=NB)[:, bass.ds(j * CB, CB), :]
                        sp.dma_start(yk[:, c, k, :, :], src).then_inc(s_y[c], 16)

                def store(j):
                    sp.dma_start(out[bass.ds(j * CB, CB), :, :].rearrange("b t d -> t b d"), chunk(x_all, j)).then_inc(s_out, 16)

                for c in range(YR):
                    load(c, c)
                with sp.Fori(0, NCH // YR - 1) as j:
                    for c in range(YR):
                        sp.wait_ge(s_sum, j * YR + (c + 1))
                        load(j * YR + (YR + c), c)
                        store(j * YR + c)
                for c in range(NCH - YR, NCH):
                    sp.wait_ge(s_sum, c + 1)
                    store(c)
                sp.wait_ge(s_out, NCH * 16)

            @block.scalar
            def _(act):
                with act.Fori(0, NCH // YR) as j:
                    for c in range(YR):
                        act.wait_ge(s_y[c], (j + 1) * (TOPK * 16))
                        for b in range(CB):
                            i = j * (YR * CB) + (c * CB + b)
                            last = act.activation(yk[:, c, 1, b, :], yk[:, c, 1, b, :], ACT.Copy, scale=gate_w[:, 1, bass.ds(i, 1)])
                        last.then_inc(s_scaled, 1)

            @block.vector
            def _(dve):
                with dve.Fori(0, NCH // YR) as j:
                    for c in range(YR):
                        dve.wait_ge(s_y[c], (j + 1) * (TOPK * 16))
                        x1 = chunk(x_all, j * YR + c)
                        for b in range(CB):
                            i = j * (YR * CB) + (c * CB + b)
                            last = dve.scalar_tensor_tensor(out=yk[:, c, 0, b, :], in0=yk[:, c, 0, b, :], scalar=gate_w[:, 0, bass.ds(i, 1)],
                                                            in1=x1[:, b, :], op0=ALU.mult, op1=ALU.add)
                        last.then_inc(s_half_sum, 1)
                        dve.wait_ge(s_half_sum, j * YR + (c + 1))
                        dve.wait_ge(s_scaled, j * YR + (c + 1))
                        dve.tensor_tensor(out=x1, in0=yk[:, c, 0, :, :], in1=yk[:, c, 1, :, :], op=ALU.add).then_inc(s_sum, 1)


_INS = ['x', 'ctx_768', 'mask_BxS2_bf1', 'g_xattn', 'g_ffn', 'L0_xattn_Wq', 'L0_xattn_Wk', 'L0_xattn_Wv', 'L0_xattn_Wo',
        'L0_ffn_Wg', 'L0_ffn_W11', 'L0_ffn_W12', 'L0_ffn_W2']


def kernel(**inputs):
    import numpy as np
    import concourse.bacc as bacc
    from concourse.bass_utils import run_bass_kernel_spmd

    nc = bacc.Bacc("TRN2", target_bir_lowering=False, num_devices=1)
    arrays, args = {}, []
    for name in _INS:
        a = np.ascontiguousarray(inputs[name])
        if a.dtype == np.bool_:
            a = a.view(np.uint8)
        if name == "ctx_768":
            a = a.transpose(0, 2, 1)
            rest = [a[:, :, KA:]] * 8
            pad = np.zeros(a.shape[:2] + (2 * P - 2 * KA - sum(r.shape[2] for r in rest),), a.dtype)
            a = np.ascontiguousarray(np.concatenate([a[:, :, :KA], a[:, :, :KA], *rest, pad], axis=2))
        arrays[f"in_{name}"] = a
        args.append(nc.dram_tensor(f"in_{name}", a.shape, mybir.dt.from_np(a.dtype), kind="ExternalInput").ap())
    shape = arrays["in_x"].shape
    args.append(nc.dram_tensor("out", shape, F32, kind="ExternalOutput").ap())
    flamingo_block(nc, *args)
    r = run_bass_kernel_spmd(nc, [arrays], core_ids=[0])
    return r.results[0]["out"]
```
